# Optimizing a Trainium2 kernel written in Bass

```python
import numpy as np
import jax
import jax.numpy as jnp

def _softmax(x, axis=-1):
    return jax.nn.softmax(x, axis=axis)

def _gelu(x):
    return jax.nn.gelu(x, approximate=True)

def _silu(x):
    return jax.nn.silu(x)

def _sigmoid(x):
    return jax.nn.sigmoid(x)

def _layernorm(x, axis=-1, eps=1e-05):
    m = jnp.mean(x, axis=axis, keepdims=True)
    v = jnp.var(x, axis=axis, keepdims=True)
    return (x - m) / jnp.sqrt(v + eps)

def _scatter_add(tgt, idx, src, axis=0):
    return tgt.at[idx].add(src)

def _segment_sum(src, seg, n):
    return jax.ops.segment_sum(src, seg, n)
kernel_name = 'mk_adj_resnorm_d4_adj_r2_859a4b'

def setup_inputs(seed: int=0):
    np.random.seed(seed)
    _w = jnp.asarray

    def _rec_inputs():
        import jax
        import jax.numpy as jnp
        _gk = jax.random.key(seed)
        x = -0.006082 + 1.001 * jax.random.normal(jax.random.fold_in(_gk, 1), (64, 128, 64), jnp.float32)
        _w = (1.0 + jnp.arange(128, dtype=jnp.float32)) ** (-0.5)
        _w = _w / _w.mean()
        _pij = jnp.clip(0.03125 * _w[:, None] * _w[None, :], 0.0, 1.0)
        _a = jax.random.uniform(jax.random.fold_in(_gk, 2), (64, 128, 128)) < _pij
        _a = jnp.logical_or(_a, jnp.swapaxes(_a, -1, -2))
        _a = jnp.logical_or(_a, jnp.eye(128, dtype=bool))
        _af = _a.astype(jnp.float32)
        _af = _af * jax.random.uniform(jax.random.fold_in(_gk, 3), (64, 128, 128), jnp.float32, 0.05, 4.42607)
        adj = _af
        _nm = jnp.ones((64, 128), dtype=bool)
        nodemask = _nm
        return (x, adj, nodemask)
    x, adj, nodemask = _rec_inputs()

    def _L0_gnn_setup():
        import jax, jax.numpy as jnp
        import numpy as np
        key = jax.random.key(seed)
        ks = jax.random.split(key, 6)
        B, N, F, H, O = (2, 256, 64, 192, 64)
        x = jax.random.normal(ks[0], (B, N, F), dtype=jnp.float32)
        adj = jax.random.normal(ks[1], (B, N, N), dtype=jnp.float32)
        W1 = jax.random.normal(ks[2], (2 * F, H), dtype=jnp.float32) * (1.0 / np.sqrt(2 * F))
        b1 = jax.random.normal(ks[3], (H,), dtype=jnp.float32) * 0.02
        W2 = jax.random.normal(ks[4], (H, O), dtype=jnp.float32) * (1.0 / np.sqrt(H))
        b2 = jax.random.normal(ks[5], (O,), dtype=jnp.float32) * 0.02
        return {'x': x, 'adj': adj, 'W1': W1, 'b1': b1, 'W2': W2, 'b2': b2}
    _L0_gnn_all = _L0_gnn_setup()
    _L0_gnn_in = {k: v for k, v in _L0_gnn_all.items() if k in ('W1', 'b1', 'W2', 'b2')}
    del _L0_gnn_all

    def _L1_gnn_setup():
        import jax, jax.numpy as jnp
        import numpy as np
        B, L, C, OUT = (32, 512, 64, 64)
        BN_EPS = 1e-05
        key = jax.random.key(seed)
        kH, kA, kW = jax.random.split(key, 3)
        H = jax.random.normal(kH, (B, L, C), dtype=jnp.float32)
        A = jax.random.uniform(kA, (B, L, L), dtype=jnp.float32)
        gamma = jnp.ones((C,), jnp.float32)
        beta = jnp.zeros((C,), jnp.float32)
        W = jax.random.normal(kW, (C, OUT), dtype=jnp.float32) * 0.05
        b = jnp.zeros((OUT,), jnp.float32)
        return {'H': H, 'A': A, 'gamma': gamma, 'beta': beta, 'W': W, 'b': b}
    _L1_gnn_all = _L1_gnn_setup()
    _L1_gnn_in = {k: v for k, v in _L1_gnn_all.items() if k in ('gamma', 'beta', 'W', 'b')}
    del _L1_gnn_all

    def _L2_gnn_setup():
        import jax, jax.numpy as jnp
        import numpy as np
        TAUS = [0.25, 0.5, 0.75]
        QWEIGHTS = [0.25, 0.5, 0.25]
        T_THRESH = 10
        K_DIL = 2
        EPS_GIN = 0.0

        def _dilate_adj(adj, mask):
            B, N, _ = adj.shape
            eye = jnp.eye(N, dtype=bool)
            adj_ = jnp.where(eye[None], 1.0, adj)
            nb = (adj_ > 0) & (~eye)[None]
            m = nb.sum(-1)
            rank = jnp.cumsum(nb, axis=-1) - 1
            skip = jnp.where(m > T_THRESH, (m + K_DIL - 1) // K_DIL, 1)
            do_dil = (skip > 1) & mask
            removed = nb & do_dil[..., None] & ((rank + 1) % skip[..., None] == 0)
            rem = removed | jnp.swapaxes(removed, 1, 2)
            return jnp.where(rem, 0.0, adj_)

        def _weighted_nanquantile_agg(x, valid):
            B, N, C = x.shape
            big = jnp.finfo(x.dtype).max / 4
            vals = jnp.where(valid[..., None], x[:, None, :, :], big)
            sv = jnp.sort(vals, axis=2)
            m = valid.sum(-1)
            mf = m.astype(x.dtype)

            def gather(idx):
                idxb = jnp.broadcast_to(idx[:, :, None, None], (B, N, 1, C))
                return jnp.take_along_axis(sv, idxb, axis=2)[:, :, 0, :]
            agg = jnp.zeros_like(x)
            for tau, wt in zip(TAUS, QWEIGHTS):
                pos = jnp.clip(tau * (mf - 1.0), 0.0)
                lo = jnp.floor(pos).astype(jnp.int32)
                hi = jnp.ceil(pos).astype(jnp.int32)
                frac = (pos - lo.astype(x.dtype))[..., None]
                q = gather(lo) * (1.0 - frac) + gather(hi) * frac
                agg = agg + wt * q
            return jnp.where((m > 0)[..., None], agg, 0.0)
        key = jax.random.key(seed)
        k0, k1, k2, k3 = jax.random.split(key, 4)
        B, N, C, H, CO = (4, 256, 64, 128, 64)
        x = jax.random.normal(k0, (B, N, C), dtype=jnp.float32)
        u = jax.random.uniform(k1, (B, N, N))
        a = (u < 0.03).astype(jnp.float32)
        adj = jnp.maximum(a, jnp.swapaxes(a, 1, 2))
        mask = jnp.broadcast_to(jnp.arange(N) < N - 32, (B, N))
        W1 = jax.random.normal(k2, (C, H), dtype=jnp.float32) * (1.0 / np.sqrt(C))
        b1 = jnp.zeros((H,), dtype=jnp.float32)
        W2 = jax.random.normal(k3, (H, CO), dtype=jnp.float32) * (1.0 / np.sqrt(H))
        b2 = jnp.zeros((CO,), dtype=jnp.float32)
        return {'x': x, 'adj': adj, 'mask': mask, 'W1': W1, 'b1': b1, 'W2': W2, 'b2': b2}
    _L2_gnn_all = _L2_gnn_setup()
    _L2_gnn_in = {k: v for k, v in _L2_gnn_all.items() if k in ('W1', 'b1', 'W2', 'b2')}
    del _L2_gnn_all

    def _L3_gnn_setup():
        import jax, jax.numpy as jnp
        import numpy as np
        B, N, H = (4, 2048, 64)
        key = jax.random.key(seed)
        ks = jax.random.split(key, 12)
        s = 1.0 / np.sqrt(H)
        h = jax.random.normal(ks[0], (B, N, H), dtype=jnp.float32)
        A = jax.random.uniform(ks[1], (B, N, N), dtype=jnp.float32)
        W1 = jax.random.normal(ks[2], (H, H), dtype=jnp.float32) * s
        b1 = jnp.zeros((H,), dtype=jnp.float32)
        W2 = jax.random.normal(ks[3], (H, H), dtype=jnp.float32) * s
        b2 = jnp.zeros((H,), dtype=jnp.float32)
        W_ih = jax.random.normal(ks[4], (3 * H, H), dtype=jnp.float32) * s
        b_ih = jnp.zeros((3 * H,), dtype=jnp.float32)
        W_hh = jax.random.normal(ks[5], (3 * H, H), dtype=jnp.float32) * s
        b_hh = jnp.zeros((3 * H,), dtype=jnp.float32)
        return {'h': h, 'A': A, 'W1': W1, 'b1': b1, 'W2': W2, 'b2': b2, 'W_ih': W_ih, 'b_ih': b_ih, 'W_hh': W_hh, 'b_hh': b_hh}
    _L3_gnn_all = _L3_gnn_setup()
    _L3_gnn_in = {k: v for k, v in _L3_gnn_all.items() if k in ('W1', 'b1', 'W2', 'b2', 'W_ih', 'b_ih', 'W_hh', 'b_hh')}
    del _L3_gnn_all
    return {'x': x, 'adj': adj, 'nodemask': nodemask, 'L0_gnn_W1': _L0_gnn_in['W1'], 'L0_gnn_b1': _L0_gnn_in['b1'], 'L0_gnn_W2': _L0_gnn_in['W2'], 'L0_gnn_b2': _L0_gnn_in['b2'], 'L1_gnn_gamma': _L1_gnn_in['gamma'], 'L1_gnn_beta': _L1_gnn_in['beta'], 'L1_gnn_W': _L1_gnn_in['W'], 'L1_gnn_b': _L1_gnn_in['b'], 'L2_gnn_W1': _L2_gnn_in['W1'], 'L2_gnn_b1': _L2_gnn_in['b1'], 'L2_gnn_W2': _L2_gnn_in['W2'], 'L2_gnn_b2': _L2_gnn_in['b2'], 'L3_gnn_W1': _L3_gnn_in['W1'], 'L3_gnn_b1': _L3_gnn_in['b1'], 'L3_gnn_W2': _L3_gnn_in['W2'], 'L3_gnn_b2': _L3_gnn_in['b2'], 'L3_gnn_W_ih': _L3_gnn_in['W_ih'], 'L3_gnn_b_ih': _L3_gnn_in['b_ih'], 'L3_gnn_W_hh': _L3_gnn_in['W_hh'], 'L3_gnn_b_hh': _L3_gnn_in['b_hh']}

def reference(x, adj, nodemask, L0_gnn_W1, L0_gnn_b1, L0_gnn_W2, L0_gnn_b2, L1_gnn_gamma, L1_gnn_beta, L1_gnn_W, L1_gnn_b, L2_gnn_W1, L2_gnn_b1, L2_gnn_W2, L2_gnn_b2, L3_gnn_W1, L3_gnn_b1, L3_gnn_W2, L3_gnn_b2, L3_gnn_W_ih, L3_gnn_b_ih, L3_gnn_W_hh, L3_gnn_b_hh):
    import jax
    import jax.numpy as jnp

    def _L0_gnn_ref(x, adj, W1, b1, W2, b2):
        import jax, jax.numpy as jnp
        import numpy as np
        F = x.shape[-1]
        mask = (adj > 0.0).astype(x.dtype)
        W1a, W1b = (W1[:F], W1[F:])
        xj_proj = x @ W1a
        diff = x[:, :, None, :] - x[:, None, :, :]
        h = jax.nn.relu(xj_proj[:, :, None, :] + diff @ W1b + b1)
        hm = jnp.einsum('bjkh,bjk->bjh', h, mask)
        deg = jnp.sum(mask, axis=-1)
        return hm @ W2 + deg[..., None] * b2

    def _L1_gnn_ref(H, A, gamma, beta, W, b):
        import jax, jax.numpy as jnp
        import numpy as np
        B, L, C, OUT = (32, 512, 64, 64)
        BN_EPS = 1e-05
        batch, l, c = H.shape
        Hf = H.reshape(batch * l, c)
        mean = Hf.mean(axis=0)
        var = jnp.mean((Hf - mean) ** 2, axis=0)
        Hn = ((Hf - mean) * jax.lax.rsqrt(var + BN_EPS) * gamma + beta).reshape(batch, l, c)
        d = A.sum(axis=2)
        A_norm = jnp.sqrt(d)[:, :, None] * A * jax.lax.rsqrt(d)[:, None, :]
        A_hat = jnp.eye(l, dtype=A.dtype) - A_norm
        X = Hn @ W + b
        out = jnp.einsum('bij,bjo->bio', A_hat, X)
        return jax.nn.leaky_relu(out, negative_slope=0.01)

    def _L2_gnn_ref(x, adj, mask, W1, b1, W2, b2):
        import jax, jax.numpy as jnp
        import numpy as np
        TAUS = [0.25, 0.5, 0.75]
        QWEIGHTS = [0.25, 0.5, 0.25]
        T_THRESH = 10
        K_DIL = 2
        EPS_GIN = 0.0

        def _dilate_adj(adj, mask):
            B, N, _ = adj.shape
            eye = jnp.eye(N, dtype=bool)
            adj_ = jnp.where(eye[None], 1.0, adj)
            nb = (adj_ > 0) & (~eye)[None]
            m = nb.sum(-1)
            rank = jnp.cumsum(nb, axis=-1) - 1
            skip = jnp.where(m > T_THRESH, (m + K_DIL - 1) // K_DIL, 1)
            do_dil = (skip > 1) & mask
            removed = nb & do_dil[..., None] & ((rank + 1) % skip[..., None] == 0)
            rem = removed | jnp.swapaxes(removed, 1, 2)
            return jnp.where(rem, 0.0, adj_)

        def _weighted_nanquantile_agg(x, valid):
            B, N, C = x.shape
            big = jnp.finfo(x.dtype).max / 4
            vals = jnp.where(valid[..., None], x[:, None, :, :], big)
            sv = jnp.sort(vals, axis=2)
            m = valid.sum(-1)
            mf = m.astype(x.dtype)

            def gather(idx):
                idxb = jnp.broadcast_to(idx[:, :, None, None], (B, N, 1, C))
                return jnp.take_along_axis(sv, idxb, axis=2)[:, :, 0, :]
            agg = jnp.zeros_like(x)
            for tau, wt in zip(TAUS, QWEIGHTS):
                pos = jnp.clip(tau * (mf - 1.0), 0.0)
                lo = jnp.floor(pos).astype(jnp.int32)
                hi = jnp.ceil(pos).astype(jnp.int32)
                frac = (pos - lo.astype(x.dtype))[..., None]
                q = gather(lo) * (1.0 - frac) + gather(hi) * frac
                agg = agg + wt * q
            return jnp.where((m > 0)[..., None], agg, 0.0)
        dtp = x.dtype
        adj_d = _dilate_adj(adj, mask)
        agg = _weighted_nanquantile_agg(x, adj_d > 0)
        out = (1.0 + EPS_GIN) * x + agg
        h = jax.nn.relu(jnp.einsum('bnc,ch->bnh', out, W1) + b1)
        y = jnp.einsum('bnh,ho->bno', h, W2) + b2
        return y * mask[..., None].astype(dtp)

    def _L3_gnn_ref(h, A, W1, b1, W2, b2, W_ih, b_ih, W_hh, b_hh):
        import jax, jax.numpy as jnp
        import numpy as np
        B, N, H = (4, 2048, 64)
        m = jax.nn.relu(jnp.einsum('bnh,hk->bnk', h, W1) + b1)
        m = jax.nn.relu(jnp.einsum('bnh,hk->bnk', m, W2) + b2)
        msg = jax.nn.relu(jnp.einsum('bij,bjh->bih', A, m))
        gi = jnp.einsum('bnh,gh->bng', msg, W_ih) + b_ih
        gh = jnp.einsum('bnh,gh->bng', h, W_hh) + b_hh
        i_r, i_z, i_n = jnp.split(gi, 3, axis=-1)
        h_r, h_z, h_n = jnp.split(gh, 3, axis=-1)
        r = jax.nn.sigmoid(i_r + h_r)
        z = jax.nn.sigmoid(i_z + h_z)
        n = jnp.tanh(i_n + r * h_n)
        return (1.0 - z) * n + z * h
    x = _layernorm(x + _L0_gnn_ref(x, adj, L0_gnn_W1, L0_gnn_b1, L0_gnn_W2, L0_gnn_b2), axis=-1)
    x = _layernorm(x + _L1_gnn_ref(x, adj, L1_gnn_gamma, L1_gnn_beta, L1_gnn_W, L1_gnn_b), axis=-1)
    x = _layernorm(x + _L2_gnn_ref(x, adj, nodemask, L2_gnn_W1, L2_gnn_b1, L2_gnn_W2, L2_gnn_b2), axis=-1)
    x = _layernorm(x + _L3_gnn_ref(x, adj, L3_gnn_W1, L3_gnn_b1, L3_gnn_W2, L3_gnn_b2, L3_gnn_W_ih, L3_gnn_b_ih, L3_gnn_W_hh, L3_gnn_b_hh), axis=-1)
    return x

_drawn_inputs = setup_inputs


def setup_inputs(seed=0):
    import zlib

    import numpy as np

    out = dict(_drawn_inputs(seed))
    spreads = {'L1_gnn_gamma': (1.0, 0.2),
     'L1_gnn_beta': (0.0, 0.1),
     'L1_gnn_b': (0.0, 0.1),
     'L2_gnn_b1': (0.0, 0.1),
     'L2_gnn_b2': (0.0, 0.1),
     'L3_gnn_b1': (0.0, 0.1),
     'L3_gnn_b2': (0.0, 0.1),
     'L3_gnn_b_ih': (0.0, 0.636),
     'L3_gnn_b_hh': (0.0, 0.8)}
    factors = {'L0_gnn_b1': 4.648, 'L0_gnn_b2': 3.058}
    for name, (base, spread) in spreads.items():
        noise = np.random.default_rng([zlib.crc32(name.encode()), seed]).standard_normal(out[name].shape)
        drawn = base * np.exp(spread * noise) if base else spread * noise
        out[name] = jnp.asarray(drawn.astype(out[name].dtype))
    for name, factor in factors.items():
        out[name] = (out[name] * factor).astype(out[name].dtype)
    return out
```

```python
from contextlib import ExitStack

import concourse.bass as bass
from concourse import mybir

F32, BF16, U8 = mybir.dt.float32, mybir.dt.bfloat16, mybir.dt.uint8
ALU, ACT, AX = mybir.AluOpType, mybir.ActivationFunctionType, mybir.AxisListType

P = 128
B = 64
C = 64
HID = 192
PAIRS = B // 2
EPS = 1e-5
TAUS = (0.25, 0.5, 0.75)
HUGE = 2.0 ** 126
TOP = 2.0 ** 127


def chain(eng, sem, start):
    n = [0]

    def link(ins):
        ins.then_inc(sem, 1)
        n[0] += 1
        eng.wait_ge(sem, start + n[0])
        return n[0]
    return link


def layer_norm(dve, link, xs, square, stat, std, ready, rooted, roots):
    wide = lambda v: v.unsqueeze(2).broadcast_to([P, B, C])
    link(dve.tensor_reduce(stat[:, 0, :], xs[:], AX.X, ALU.add))
    link(dve.tensor_scalar(stat[:, 0, :], stat[:, 0, :], 1.0 / C, None, ALU.mult))
    link(dve.tensor_tensor(out=xs[:], in0=xs[:], in1=wide(stat[:, 0, :]), op=ALU.subtract))
    link(dve.tensor_tensor(out=square[:], in0=xs[:], in1=xs[:], op=ALU.mult))
    link(dve.tensor_reduce(stat[:, 0, :], square[:], AX.X, ALU.add))
    dve.tensor_scalar(stat[:, 1, :], stat[:, 0, :], 1.0 / C, EPS, ALU.mult, ALU.add).then_inc(ready, 1)
    dve.wait_ge(rooted, roots)
    link(dve.reciprocal(stat[:, 0, :], std[:]))
    link(dve.tensor_tensor(out=xs[:], in0=xs[:], in1=wide(stat[:, 0, :]), op=ALU.mult))


def neighbours(nc, t, adj, adjT, mask, x, ident):
    G = 8
    CH = B // G
    with ExitStack() as ctx:
        sb = lambda n, s, d: ctx.enter_context(nc.sbuf_tensor(n, s, d))
        pb = lambda n, s, d: ctx.enter_context(nc.psum_tensor(n, s, d))
        sem = lambda n: ctx.enter_context(nc.semaphore(n))
        adjc = sb("adjc", [P, 2, G, P], F32)
        pos, nb, rank, t1, first, both = (sb(n, [P, G, P], F32) for n in ("pos", "nb", "rank", "t1", "first", "both"))
        zero = sb("zero", [P, G * P], F32)
        m, even, cut, basis = (sb(n, [P, G], F32) for n in ("m", "even", "cut", "basis"))
        rem, sym, a1 = (sb(n, [P, G, P], BF16) for n in ("rem", "sym", "a1"))
        noteye = sb("noteye", [P, P], F32)
        mask8 = sb("mask8", [P, B], U8)
        remT = pb("remT", [P, G, P], BF16)
        loaded, work, turned = sem("n_loaded"), sem("n_work"), sem("n_turned")
        chunk_in = [sem("n_chunk_in0"), sem("n_chunk_in1")]
        OPS, SETUP, REM_AT, ADJ_AT = 21, 7, 18, 2
        block = ctx.enter_context(nc.Block())

        @block.sync
        def _(sp):
            sp.dma_start(t.eye[:], ident).then_inc(loaded, 16)
            sp.dma_start(mask8[:], mask).then_inc(loaded, 16)
            sp.dma_start(adjc[:, 0], adj[:, 0:G]).then_inc(chunk_in[0], 16)
            sp.dma_start(adjc[:, 1], adj[:, G:2 * G]).then_inc(chunk_in[1], 16)
            sp.dma_start(t.xs[:], x).then_inc(loaded, 16)
            sp.dma_start(t.adjT[:], adjT).then_inc(loaded, 16)
            with sp.Fori(1, CH // 2) as i:
                for p in range(2):
                    sp.wait_ge(work, SETUP + (2 * i + p - 2) * OPS + OPS)
                    sp.dma_start(adjc[:, p], adj[:, bass.ds((2 * i + p) * G, G)]).then_inc(chunk_in[p], 16)

        @block.vector
        def _(dve):
            link = chain(dve, work, 0)
            link(dve.memset(zero[:], 0.0))
            link(dve.memset(basis[:], 0.0))
            link(dve.memset(t.ones[:], 1.0))
            link(dve.memset(t.onesf[:], 1.0))
            dve.wait_ge(loaded, 64)
            link(dve.tensor_copy(t.maskf[:], mask8[:]))
            link(dve.tensor_copy(t.eyeb[:], t.eye[:]))
            assert link(dve.tensor_scalar(noteye[:], t.eye[:], -1.0, 1.0, ALU.mult, ALU.add)) == SETUP
            wide = lambda v: v.unsqueeze(2).broadcast_to([P, G, P])
            over = lambda v: v.unsqueeze(1).broadcast_to([P, G, P])
            with dve.Fori(0, CH // 2) as i:
                for p in range(2):
                    j = 2 * i + p
                    here = bass.ds(j * G, G)
                    link = chain(dve, work, SETUP + j * OPS)
                    dve.wait_ge(chunk_in[p], 16 * (i + 1))
                    link(dve.tensor_reduce(t.rowsum[:, here], adjc[:, p], AX.X, ALU.add))
                    link(dve.tensor_scalar(pos[:], adjc[:, p], 0.0, None, ALU.is_gt))
                    link(dve.tensor_reduce(t.degree[:, here], pos[:], AX.X, ALU.add))
                    link(dve.tensor_tensor(out=nb[:], in0=pos[:], in1=over(noteye[:]), op=ALU.mult))
                    link(dve.tensor_reduce(m[:], nb[:], AX.X, ALU.add))
                    link(dve.tensor_tensor_scan(rank[:].rearrange("p g k -> p (g k)"), nb[:].rearrange("p g k -> p (g k)"),
                                                zero[:], 0.0, ALU.add, ALU.add))
                    link(dve.tensor_copy(basis[:, 1:G], rank[:, 0:G - 1, P - 1]))
                    link(dve.tensor_tensor(out=rank[:], in0=rank[:], in1=wide(basis[:]), op=ALU.subtract))
                    link(dve.scalar_tensor_tensor(out=t1[:], in0=rank[:], scalar=2.0, in1=wide(m[:]), op0=ALU.mult, op1=ALU.subtract))
                    link(dve.scalar_tensor_tensor(out=first[:], in0=t1[:], scalar=0.0, in1=nb[:], op0=ALU.is_equal, op1=ALU.mult))
                    link(dve.tensor_reduce(even[:], first[:], AX.X, ALU.max))
                    link(dve.scalar_tensor_tensor(out=both[:], in0=t1[:], scalar=1.0, in1=first[:], op0=ALU.is_equal, op1=ALU.add))
                    link(dve.tensor_tensor(out=t1[:], in0=rank[:], in1=wide(m[:]), op=ALU.is_equal))
                    link(dve.tensor_tensor(out=t1[:], in0=t1[:], in1=wide(even[:]), op=ALU.mult))
                    link(dve.tensor_tensor(out=both[:], in0=both[:], in1=t1[:], op=ALU.add))
                    link(dve.scalar_tensor_tensor(out=cut[:], in0=m[:], scalar=10.0, in1=t.maskf[:, here], op0=ALU.is_gt, op1=ALU.mult))
                    link(dve.tensor_tensor(out=both[:], in0=both[:], in1=nb[:], op=ALU.mult))
                    assert link(dve.tensor_tensor(out=rem[:], in0=both[:], in1=wide(cut[:]), op=ALU.mult)) == REM_AT
                    link(dve.scalar_tensor_tensor(out=a1[:], in0=t.adjT[:, here], scalar=0.0, in1=over(t.eye[:]), op0=ALU.is_gt, op1=ALU.max))
                    dve.wait_ge(turned, j + 1)
                    link(dve.tensor_tensor(out=sym[:], in0=rem[:], in1=remT[:], op=ALU.max))
                    assert link(dve.scalar_tensor_tensor(out=t.negV[:, here], in0=sym[:], scalar=1.0, in1=a1[:],
                                                         op0=ALU.subtract, op1=ALU.mult)) == OPS

        @block.tensor
        def _(pe):
            with pe.Fori(0, CH) as j:
                pe.wait_ge(work, SETUP + j * OPS + REM_AT)
                for g in range(G):
                    last = pe.transpose(remT[:, g], rem[:, g], t.eyeb[:])
                last.then_inc(turned, 1)


BANKS = HID // 4
KINDS = "DADAADADAADA"
DONE = {k: [sum(KINDS[b % 12] == k for b in range(n)) for n in range(BANKS + 1)] for k in "DA"}
A_LAG = 2
ORDER = sorted(range(BANKS), key=lambda b: b + (A_LAG + 0.5 if KINDS[b % 12] == "A" else 0))
RING, CMPS, SIGNS = 4, 6, 4
RED_LAG = 3


def edge_mlp(nc, t, xT, W1, b1):
    with ExitStack() as ctx:
        sb = lambda n, s, d: ctx.enter_context(nc.sbuf_tensor(n, s, d))
        pb = lambda n, s, d: ctx.enter_context(nc.psum_tensor(n, s, d))
        sem = lambda n: ctx.enter_context(nc.semaphore(n))
        w1 = sb("w1", [C, 2, HID], F32)
        wuv = sb("wuv", [C + 1, 2 * HID], F32)
        xTg = sb("xTg", [C + 1, 2, P], F32)
        uv = sb("uv", [P, 2, 2 * HID], F32)
        negv = sb("negv", [P, 2, HID], F32)
        uT = sb("uT", [P, 2, P], F32)
        uTparts = sb("uTparts", [P, 2, 3, 2, P], BF16)
        ru = sb("ru", [P, 2, P], F32)
        rv = sb("rv", [P, HID], F32)
        one_v = sb("one_v", [P, 2, HID, 4], BF16)
        rows = sb("rows", [2 * 32 + 3, 2, 64 * P], BF16)
        far = sb("far", [P, 2, P], BF16)
        away = sb("away", [P, 2, P], BF16)
        signs = sb("signs", [P, SIGNS, 4, P], BF16)
        cmps = sb("cmps", [P, CMPS, 4, P], BF16)
        sums = sb("sums", [P, HID, 4], F32)
        part = sb("part", [P, HID], F32)
        nil = sb("nil", [P, 2, P], F32)
        nil_v = nil[:].rearrange("p a k -> p (a k)")[:, 0:HID]
        bank = pb("bank", [P, RING, 4, P], F32)
        red = pb("red", [P, HID, 4], F32)
        uvp = pb("uvp", [P, 512], F32)
        uTp = pb("uTp", [P, 2, P], F32)
        w_in, set_, uv_ps, uv_sb, pool = (sem("e_" + n) for n in ("w_in", "set", "uv_ps", "uv_sb", "pool"))
        x_in, rows_in = ([sem(f"e_{n}{p}") for p in range(2)] for n in ("x_in", "rows_in"))
        masked, bcast, compared, signed, cmp_done, reduced, sums_done, set_act = (
            sem("e_" + n) for n in ("masked", "bcast", "compared", "signed", "cmp_done", "reduced", "sums_done", "set_act"))
        set_gp = sem("e_set_gp")
        POOL = 14
        block = ctx.enter_context(nc.Block())

        def pair_loop(eng, body):
            body(0)
            with eng.Fori(1, PAIRS - 1) as i:
                body(i)
            body(PAIRS - 1)

        def after(eng, sem_, g, per, n):
            v = g * per + n
            if not isinstance(v, int) or v > 0:
                eng.wait_ge(sem_, v)

        @block.sync
        def _(sp):
            sp.dma_start(w1[:], W1).then_inc(w_in, 16)
            sp.dma_start(wuv[C:C + 1, 0:HID], b1).then_inc(w_in, 16)

            def load(i, p):
                g = 2 * i + p
                after(sp, uv_ps, g - 2, 1, 1)
                sp.dma_start(xTg[0:C, p], xT[:, bass.ds(g * P, P)]).then_inc(x_in[p], 16)

            def flatten(i, p):
                g = 2 * i + p
                sp.wait_ge(pool, g * POOL + 5)
                after(sp, bcast, g - 2, BANKS, BANKS)
                for s in range(3):
                    for q in range(3):
                        src = uTparts[64 * (q % 2):64 * (q % 2) + 64, p, s, q // 2, :]
                        sp.dma_start(rows[32 * q + s:32 * q + s + 1, p, :].rearrange("o (h k) -> o h k", h=64),
                                     src).then_inc(rows_in[p], 16)

            load(0, 0)
            load(0, 1)
            flatten(0, 0)

            def body(i):
                for p in range(2):
                    g = 2 * i + p
                    last = isinstance(i, int) and i == PAIRS - 1
                    if not (last):
                        load(i + 1, p)
                    if not (last and p == 1):
                        flatten(i + p, 1 - p)
            pair_loop(sp, body)

        @block.gpsimd
        def _(gp):
            gp.memset(one_v[:], 1.0).then_inc(set_gp, 1)
            gp.wait_ge(set_gp, 1)
            gp.memset(uT[64:P, 1, :], 0.0).then_inc(set_gp, 1)
            gp.wait_ge(set_gp, 2)
            gp.memset(nil[:], 0.0).then_inc(set_gp, 1)
            gp.wait_ge(set_gp, 3)

            def parts(i, p):
                g = 2 * i + p
                link = chain(gp, pool, g * POOL)
                gp.wait_ge(uv_sb, 3 * (g + 1))
                after(gp, rows_in[p], i, 144, 0)
                link(gp.tensor_tensor(out=uTparts[:, p, 0], in0=uT[:], in1=nil[:], op=ALU.add))
                link(gp.tensor_tensor(out=ru[:], in0=uT[:], in1=uTparts[:, p, 0], op=ALU.subtract))
                link(gp.tensor_tensor(out=uTparts[:, p, 1], in0=ru[:], in1=nil[:], op=ALU.add))
                link(gp.tensor_tensor(out=ru[:], in0=ru[:], in1=uTparts[:, p, 1], op=ALU.subtract))
                link(gp.tensor_tensor(out=uTparts[:, p, 2], in0=ru[:], in1=nil[:], op=ALU.add))
                after(gp, reduced, g - 2, BANKS, BANKS)
                v = uv[:, p, HID:2 * HID]
                link(gp.tensor_tensor(out=one_v[:, p, :, 1], in0=v, in1=nil_v, op=ALU.add))
                link(gp.tensor_tensor(out=rv[:], in0=v, in1=one_v[:, p, :, 1], op=ALU.subtract))
                link(gp.tensor_tensor(out=one_v[:, p, :, 2], in0=rv[:], in1=nil_v, op=ALU.add))
                link(gp.tensor_tensor(out=rv[:], in0=rv[:], in1=one_v[:, p, :, 2], op=ALU.subtract))
                link(gp.tensor_tensor(out=one_v[:, p, :, 3], in0=rv[:], in1=nil_v, op=ALU.add))

            def finish(g, p):
                link = chain(gp, pool, (g + 1) * POOL + (10 if not (isinstance(g, int) and g == B - 1) else 0))
                gp.wait_ge(sums_done, g + 1)
                link(gp.tensor_tensor(out=part[:], in0=sums[:, :, 3], in1=sums[:, :, 2], op=ALU.add))
                link(gp.tensor_tensor(out=part[:], in0=part[:], in1=sums[:, :, 1], op=ALU.add))
                link(gp.tensor_tensor(out=rv[:], in0=sums[:, :, 0], in1=uv[:, p, 0:HID], op=ALU.mult))
                link(gp.tensor_tensor(out=t.hm[:, bass.ds(g, 1), :].rearrange("p o h -> p (o h)"), in0=rv[:], in1=part[:], op=ALU.subtract))

            parts(0, 0)
            gp.memset(part[:], 0.0).then_inc(pool, 4)
            gp.wait_ge(pool, POOL)

            def body(i):
                for p in range(2):
                    g = 2 * i + p
                    if not (isinstance(i, int) and i == PAIRS - 1 and p == 1):
                        parts(i + p, 1 - p)
                    finish(g, p)
            pair_loop(gp, body)

        @block.scalar
        def _(act):
            def spread(i, p):
                g = 2 * i + p
                act.wait_ge(uv_ps, g + 1)
                after(act, compared, g - 2, DONE["D"][BANKS], DONE["D"][BANKS])
                after(act, pool, g, POOL, 0)
                after(act, signed, g - 2, DONE["A"][BANKS], DONE["A"][BANKS])
                act.copy(uv[:, p], uvp[:, 0:2 * HID]).then_inc(uv_sb, 1)
                act.mul(negv[:, p], uvp[:, HID:2 * HID], -1.0).then_inc(set_act, 1)
                act.copy(uT[:, 0], uTp[:, 0]).then_inc(uv_sb, 1)
                act.copy(uT[0:64, 1], uTp[0:64, 1]).then_inc(uv_sb, 1)

            act.wait_ge(set_gp, 3)
            spread(0, 0)

            def body(i):
                for p in range(2):
                    g = 2 * i + p
                    act.wait_ge(set_act, g + 1)
                    for b in range(BANKS):
                        if KINDS[b % 12] == "D":
                            continue
                        n = DONE["A"][b]
                        act.wait_ge(bcast, g * BANKS + b + 1)
                        after(act, cmp_done, g, DONE["A"][BANKS], n - SIGNS + 1)
                        for h in range(4):
                            ins = act.activation(signs[:, n % SIGNS, h], bank[:, b % RING, h], ACT.Sign,
                                                 bias=negv[:, p, 4 * b + h:4 * b + h + 1])
                        ins.then_inc(signed, 1)
                        if b > 12 and DONE["A"][b] == DONE["A"][24] and not (isinstance(i, int) and i == PAIRS - 1 and p == 1):
                            spread(i + p, 1 - p)
                    act.wait_ge(reduced, (g + 1) * BANKS)
                    after(act, pool, g, POOL, POOL)
                    act.copy(sums[:], red[:]).then_inc(sums_done, 1)
            pair_loop(act, body)

        @block.vector
        def _(dve):
            dve.wait_ge(w_in, 32)
            dve.tensor_tensor(out=wuv[0:C, 0:HID], in0=w1[:, 0], in1=w1[:, 1], op=ALU.add).then_inc(set_, 1)
            dve.tensor_copy(wuv[0:C, HID:2 * HID], w1[:, 1]).then_inc(set_, 1)
            dve.memset(wuv[C:C + 1, HID:2 * HID], 0.0).then_inc(set_, 1)
            dve.memset(xTg[C:C + 1], 1.0).then_inc(set_, 1)

            def masks(i, p):
                g = 2 * i + p
                after(dve, bcast, g - 2, BANKS, BANKS)
                after(dve, cmp_done, g - 2, DONE["A"][BANKS], DONE["A"][BANKS])
                a = t.adjT[:, bass.ds(g, 1), :].rearrange("p o k -> p (o k)")
                dve.tensor_scalar(away[:, p], a, 0.0, -HUGE, ALU.is_le, ALU.mult).then_inc(masked, 1)
                dve.tensor_scalar(far[:, p], a, 0.0, None, ALU.is_le).then_inc(masked, 1)

            masks(0, 0)

            def body(i):
                for p in range(2):
                    g = 2 * i + p
                    dve.wait_ge(uv_sb, 3 * g + 1)
                    dve.wait_ge(masked, 2 * (g + 1))
                    for n, b in enumerate(ORDER):
                        cmp = cmps[:, n % CMPS]
                        after(dve, reduced, g, BANKS, n - CMPS + 1)
                        if KINDS[b % 12] == "D":
                            dve.wait_ge(bcast, g * BANKS + b + 1)
                            v = uv[:, p, HID + 4 * b:HID + 4 * b + 4].unsqueeze(2).broadcast_to([P, 4, P])
                            ins = dve.tensor_tensor(out=cmp, in0=bank[:, b % RING], in1=v, op=ALU.is_gt)
                            ins.then_inc(compared, 1)
                        else:
                            dve.wait_ge(signed, g * DONE["A"][BANKS] + DONE["A"][b] + 1)
                            f = far[:, p].unsqueeze(1).broadcast_to([P, 4, P])
                            ins = dve.tensor_tensor(out=cmp, in0=signs[:, DONE["A"][b] % SIGNS], in1=f, op=ALU.is_gt)
                            ins.then_inc(cmp_done, 1)
                        if n == 24 and not (isinstance(i, int) and i == PAIRS - 1 and p == 1):
                            masks(i + p, 1 - p)
            pair_loop(dve, body)

        @block.tensor
        def _(pe):
            def project(i, p):
                g = 2 * i + p
                pe.wait_ge(x_in[p], 16 * (i + 1))
                after(pe, uv_sb, g, 3, 0)
                after(pe, set_act, g, 1, 0)
                pe.matmul(uvp[:, 0:2 * HID], xTg[:, p], wuv[:], start=True, stop=True)
                pe.matmul(uTp[:, 0], wuv[:, 0:P], xTg[:, p], start=True, stop=True)
                pe.matmul(uTp[0:64, 1], wuv[:, P:HID], xTg[:, p], start=True, stop=True).then_inc(uv_ps, 1)

            pe.wait_ge(w_in, 32)
            pe.wait_ge(set_, 4)
            pe.wait_ge(set_gp, 3)
            project(0, 0)

            def reduce(g, p, n):
                b = ORDER[n]
                k = KINDS[b % 12]
                pe.wait_ge(compared if k == "D" else cmp_done, g * DONE[k][BANKS] + DONE[k][b] + 1)
                if n == 0:
                    pe.wait_ge(pool, g * POOL + 10)
                    after(pe, sums_done, g, 1, 0)
                for h in range(4):
                    ins = pe.matmul(red[:, 4 * b + h], cmps[:, n % CMPS, h], one_v[:, p, 4 * b + h], start=True, stop=True)
                ins.then_inc(reduced, 1)

            def body(i):
                for p in range(2):
                    g = 2 * i + p
                    pe.wait_ge(rows_in[p], 144 * (i + 1))
                    pe.wait_ge(masked, 2 * (g + 1))
                    for b in range(BANKS + RED_LAG):
                        if b < BANKS:
                            k = KINDS[(b - RING) % 12]
                            after(pe, compared if k == "D" else signed, g, DONE[k][BANKS],
                                  DONE[k][b - RING] + 1 if b >= RING else DONE[k][b - RING + BANKS] + 1 - DONE[k][BANKS])
                            q, c = divmod(4 * b, 64)
                            mine = KINDS[b % 12] == "D"
                            ins = pe.matmul(bank[:, b % RING], t.ones[32 * q:32 * q + 3, :], rows[32 * q:32 * q + 3, p, c * P:(c + 4) * P],
                                            start=True, stop=not mine)
                            if mine:
                                ins = pe.matmul(bank[:, b % RING], t.eyeb[:], away[:, p].unsqueeze(1).broadcast_to([P, 4, P]),
                                                start=False, stop=True)
                            ins.then_inc(bcast, 1)
                        if b >= RED_LAG:
                            reduce(g, p, b - RED_LAG)
                        if b == 30 and not (isinstance(i, int) and i == PAIRS - 1 and p == 1):
                            project(i + p, 1 - p)
            pair_loop(pe, body)


def edge_out(nc, t, W2, b2):
    N = 4
    with ExitStack() as ctx:
        sb = lambda n, s, d: ctx.enter_context(nc.sbuf_tensor(n, s, d))
        pb = lambda n, s, d: ctx.enter_context(nc.psum_tensor(n, s, d))
        sem = lambda n: ctx.enter_context(nc.semaphore(n))
        w2 = sb("w2", [P, 2, C], F32)
        b2b = sb("b2b", [P, C], F32)
        stage = sb("stage", [P, 2, N, HID], F32)
        nil = sb("nilo", [P, N, HID], F32)
        set_gp, biased = sem("o_set_gp"), sem("o_biased")
        hT = sb("hT", [P, 2, N, P], F32)
        square = sb("square", [P, B, C], F32)
        stat, std = sb("stat", [P, 2, B], F32), sb("std", [P, B], F32)
        hTp = pb("hTp", [P, 2, 2, N, P], F32)
        y = pb("y", [P, 2, 512], F32)
        w_in, staged, turned, copied, made, work, ready, rooted = (
            sem("o_" + n) for n in ("w_in", "staged", "turned", "copied", "made", "work", "ready", "rooted"))
        block = ctx.enter_context(nc.Block())

        @block.sync
        def _(sp):
            sp.dma_start(w2[:, 0], W2[0:P]).then_inc(w_in, 16)
            sp.dma_start(w2[0:C, 1], W2[P:HID]).then_inc(w_in, 16)
            sp.dma_start(b2b[:], b2).then_inc(w_in, 16)

        def rounds(eng, body):
            for j in range(2):
                body(j, j)
            with eng.Fori(1, B // N // 2) as i:
                for p in range(2):
                    body(2 * i + p, p)

        @block.gpsimd
        def _(gp):
            gp.memset(nil[:], 0.0).then_inc(set_gp, 1)
            gp.wait_ge(set_gp, 1)

            def body(j, p):
                if not isinstance(j, int):
                    gp.wait_ge(turned, j - 1)
                gp.tensor_tensor(out=stage[:, p], in0=t.hm[:, bass.ds(j * N, N)], in1=nil[:], op=ALU.add).then_inc(staged, 1)
            rounds(gp, body)

        @block.tensor
        def _(pe):
            pe.wait_ge(w_in, 48)

            def body(j, p):
                pe.wait_ge(staged, j + 1)
                if not isinstance(j, int):
                    pe.wait_ge(copied, 2 * (j - 1))
                for g in range(N):
                    pe.transpose(hTp[:, p, 0, g], stage[:, p, g, 0:P], t.eye[:])
                    last = pe.transpose(hTp[0:C, p, 1, g], stage[:, p, g, P:HID], t.eye[:])
                last.then_inc(turned, 1)
                pe.wait_ge(copied, 2 * (j + 1))
                if not isinstance(j, int):
                    pe.wait_ge(work, 2 * (j - 1))
                for g in range(N):
                    pe.matmul(y[:, p, g * C:(g + 1) * C], hT[:, 0, g], w2[:, 0], start=True, stop=False)
                    last = pe.matmul(y[:, p, g * C:(g + 1) * C], hT[0:C, 1, g], w2[0:C, 1], start=False, stop=True)
                last.then_inc(made, 1)
            rounds(pe, body)

        @block.scalar
        def _(act):
            def body(j, p):
                act.wait_ge(turned, j + 1)
                if not (isinstance(j, int) and j == 0):
                    act.wait_ge(made, j)
                act.copy(hT[:, 0], hTp[:, p, 0]).then_inc(copied, 1)
                act.copy(hT[0:C, 1], hTp[0:C, p, 1]).then_inc(copied, 1)
            rounds(act, body)
            act.wait_ge(ready, 1)
            act.activation(std[:], stat[:, 1, :], ACT.Sqrt).then_inc(rooted, 1)

        @block.vector
        def _(dve):
            dve.wait_ge(w_in, 48)

            def body(j, p):
                link = chain(dve, work, 2 * j)
                here = bass.ds(j * N, N)
                if isinstance(j, int) and j == 0:
                    db = dve.tensor_tensor(out=square[:], in0=b2b[:].unsqueeze(1).broadcast_to([P, B, C]),
                                           in1=t.degree[:].unsqueeze(2).broadcast_to([P, B, C]), op=ALU.mult)
                    db.then_inc(biased, 1)
                    dve.wait_ge(biased, 1)
                link(dve.tensor_tensor(out=t.xs[:, here], in0=t.xs[:, here], in1=square[:, here], op=ALU.add))
                dve.wait_ge(made, j + 1)
                link(dve.tensor_tensor(out=t.xs[:, here], in0=t.xs[:, here],
                                       in1=y[:, p, 0:N * C].rearrange("p (g c) -> p g c", g=N), op=ALU.add))
            rounds(dve, body)
            link = chain(dve, work, 2 * (B // N))
            layer_norm(dve, link, t.xs, square, stat, std, ready, rooted, 1)


def rounds(eng, n, body):
    for j in range(2):
        body(j, j)
    with eng.Fori(1, n // 2) as i:
        for p in range(2):
            body(2 * i + p, p)


def at_least(eng, sem, v):
    if not isinstance(v, int) or v > 0:
        eng.wait_ge(sem, v)


def graph_conv(nc, t, W, gamma, beta, b):
    N = 4
    ROUNDS = B // N
    with ExitStack() as ctx:
        sb = lambda n, s, d: ctx.enter_context(nc.sbuf_tensor("c_" + n, s, d))
        pb = lambda n, s, d: ctx.enter_context(nc.psum_tensor("c_" + n, s, d))
        sem = lambda n: ctx.enter_context(nc.semaphore("c_" + n))
        w = sb("w", [P, 2, C], F32)
        gammab, betab, bb = (sb(n, [P, C], F32) for n in ("gamma", "beta", "bb"))
        hn, square = sb("hn", [P, B, C], F32), sb("square", [P, B, C], F32)
        stat, std = sb("stat", [P, 2, B], F32), sb("std", [P, B], F32)
        norm, nstd = sb("norm", [P, 2, C], F32), sb("nstd", [P, C], F32)
        root, iroot = sb("root", [P, B], F32), sb("iroot", [P, B], F32)
        hstage = sb("hstage", [P, 2, N, C], F32)
        astage = sb("astage", [P, 2, N, P], F32)
        nil = sb("nil", [P, N, P], F32)
        hT = sb("hT", [P, 2, N // 2, P], F32)
        xw, yw, z2 = sb("xw", [P, 2, N, C], F32), sb("yw", [P, 2, N, C], F32), sb("z2", [P, N, C], F32)
        sump = pb("sump", [P, 8, C], F32)
        hTp = pb("hTp", [P, 2, 512], F32)
        xp, zp = pb("xp", [P, 2, 512], F32), pb("zp", [P, 2, 512], F32)
        w_in, set_gp, work, summed, ready, rooted, staged, turned, copied, made_x, made_y, made_z, done, biased, added, set_w = (
            sem(n) for n in ("w_in", "set_gp", "work", "summed", "ready", "rooted", "staged", "turned", "copied",
                             "made_x", "made_y", "made_z", "done", "biased", "added", "set_w"))
        block = ctx.enter_context(nc.Block())

        @block.sync
        def _(sp):
            sp.wait_ge(set_w, 1)
            for h in range(2):
                sp.dma_start(w[C * h:C * h + C, h], W).then_inc(w_in, 16)
            for dst, src in ((gammab, gamma), (betab, beta), (bb, b)):
                sp.dma_start(dst[:], src).then_inc(w_in, 16)

        @block.gpsimd
        def _(gp):
            gp.memset(nil[:], 0.0).then_inc(set_gp, 1)
            gp.wait_ge(set_gp, 1)
            gp.wait_ge(work, 10)

            def body(j, p):
                at_least(gp, turned, j - 1)
                gp.tensor_tensor(out=hstage[:, p], in0=hn[:, bass.ds(j * N, N)], in1=nil[:, :, 0:C], op=ALU.add).then_inc(staged, 1)
                at_least(gp, made_z, j - 1)
                gp.tensor_tensor(out=astage[:, p], in0=t.adjT[:, bass.ds(j * N, N)], in1=nil[:], op=ALU.add).then_inc(staged, 1)
            rounds(gp, ROUNDS, body)

        @block.tensor
        def _(pe):
            for j in range(8):
                last = pe.matmul(sump[:], t.onesf[:], t.xs[:, 8 * j:8 * j + 8], start=(j == 0), stop=(j == 7))
            last.then_inc(summed, 1)
            pe.wait_ge(work, 4)
            for j in range(8):
                last = pe.matmul(sump[:], t.onesf[:], square[:, 8 * j:8 * j + 8], start=(j == 0), stop=(j == 7))
            last.then_inc(summed, 1)
            pe.wait_ge(w_in, 80)

            def neighbours_sum(j, p):
                pe.wait_ge(made_y, j + 1)
                at_least(pe, done, j - 1)
                for g in range(N):
                    last = pe.matmul(zp[:, p, g * C:(g + 1) * C], astage[:, p, g], yw[:, p, g], start=True, stop=True)
                last.then_inc(made_z, 1)

            def body(j, p):
                pe.wait_ge(staged, 2 * (j + 1))
                at_least(pe, copied, j - 1)
                for g in range(N // 2):
                    last = pe.transpose(hTp[:, p, g * P:(g + 1) * P], hstage[:, p, 2 * g:2 * g + 2].rearrange("p g c -> p (g c)"), t.eye[:])
                last.then_inc(turned, 1)
                pe.wait_ge(copied, j + 1)
                at_least(pe, made_y, j - 1)
                for g in range(N // 2):
                    last = pe.matmul(xp[:, p, g * P:(g + 1) * P], hT[:, p, g], w[:], start=True, stop=True)
                last.then_inc(made_x, 1)
                if not (isinstance(j, int) and j == 0):
                    neighbours_sum(j - 1, 1 - p)
            rounds(pe, ROUNDS, body)
            neighbours_sum(ROUNDS - 1, (ROUNDS - 1) % 2)

        @block.scalar
        def _(act):
            act.activation(root[:], t.rowsum[:], ACT.Sqrt).then_inc(rooted, 1)
            act.wait_ge(ready, 1)
            act.activation(nstd[:], norm[:, 1], ACT.Sqrt).then_inc(rooted, 1)

            def body(j, p):
                act.wait_ge(turned, j + 1)
                at_least(act, made_x, j - 1)
                act.copy(hT[:, p].rearrange("p g k -> p (g k)"), hTp[:, p, 0:N // 2 * P]).then_inc(copied, 1)
            rounds(act, ROUNDS, body)
            act.wait_ge(ready, 2)
            act.activation(std[:], stat[:, 1, :], ACT.Sqrt).then_inc(rooted, 1)

        @block.vector
        def _(dve):
            dve.memset(w[:], 0.0).then_inc(set_w, 1)
            link = chain(dve, work, 0)
            by_channel = lambda v: v.rearrange("p g c -> p c g")
            over = lambda v: v.unsqueeze(1).broadcast_to([P, B, C])
            dve.wait_ge(summed, 1)
            link(dve.tensor_reduce(norm[:, 0], by_channel(sump[:]), AX.X, ALU.add))
            link(dve.tensor_scalar(norm[:, 0], norm[:, 0], 1.0 / (B * P), None, ALU.mult))
            link(dve.tensor_tensor(out=hn[:], in0=t.xs[:], in1=over(norm[:, 0]), op=ALU.subtract))
            link(dve.tensor_tensor(out=square[:], in0=hn[:], in1=hn[:], op=ALU.mult))
            dve.wait_ge(summed, 2)
            link(dve.tensor_reduce(norm[:, 0], by_channel(sump[:]), AX.X, ALU.add))
            dve.tensor_scalar(norm[:, 1], norm[:, 0], 1.0 / (B * P), EPS, ALU.mult, ALU.add).then_inc(ready, 1)
            dve.wait_ge(rooted, 2)
            dve.wait_ge(w_in, 80)
            link(dve.reciprocal(norm[:, 0], nstd[:]))
            link(dve.tensor_tensor(out=norm[:, 0], in0=norm[:, 0], in1=gammab[:], op=ALU.mult))
            link(dve.tensor_tensor(out=hn[:], in0=hn[:], in1=over(norm[:, 0]), op=ALU.mult))
            link(dve.reciprocal(iroot[:], root[:]))
            assert link(dve.tensor_tensor(out=hn[:], in0=hn[:], in1=over(betab[:]), op=ALU.add)) == 10
            wide = lambda v: v.unsqueeze(2).broadcast_to([P, N, C])

            def scale_in(j, p):
                dve.wait_ge(made_x, j + 1)
                if not (isinstance(j, int) and j < 2):
                    dve.wait_ge(done, j - 1)
                x = dve.tensor_tensor(out=xw[:, p], in0=xp[:, p, 0:N * C].rearrange("p (g c) -> p g c", g=N),
                                      in1=bb[:].unsqueeze(1).broadcast_to([P, N, C]), op=ALU.add)
                x.then_inc(biased, 1)
                dve.wait_ge(biased, j + 1)
                at_least(dve, made_z, j - 1)
                dve.tensor_tensor(out=yw[:, p], in0=xw[:, p], in1=wide(iroot[:, bass.ds(j * N, N)]), op=ALU.mult).then_inc(made_y, 1)

            def add_up(j, p):
                link = chain(dve, added, 3 * j)
                here = bass.ds(j * N, N)
                dve.wait_ge(made_z, j + 1)
                link(dve.tensor_tensor(out=z2[:], in0=zp[:, p, 0:N * C].rearrange("p (g c) -> p g c", g=N),
                                       in1=wide(root[:, here]), op=ALU.mult))
                link(dve.tensor_tensor(out=z2[:], in0=xw[:, p], in1=z2[:], op=ALU.subtract))
                link(dve.scalar_tensor_tensor(out=z2[:], in0=z2[:], scalar=0.01, in1=z2[:], op0=ALU.mult, op1=ALU.max))
                dve.tensor_tensor(out=t.xs[:, here], in0=t.xs[:, here], in1=z2[:], op=ALU.add).then_inc(done, 1)
                dve.wait_ge(done, j + 1)

            def body(j, p):
                scale_in(j, p)
                if not (isinstance(j, int) and j == 0):
                    add_up(j - 1, 1 - p)
            rounds(dve, ROUNDS, body)
            add_up(ROUNDS - 1, (ROUNDS - 1) % 2)
            link = chain(dve, work, 10)
            layer_norm(dve, link, t.xs, square, stat, std, ready, rooted, 3)


def sort_columns(nc, t):
    TURNS = PAIRS // 2
    LOW = -3.0e38
    with ExitStack() as ctx:
        sb = lambda n, s, d: ctx.enter_context(nc.sbuf_tensor("s_" + n, s, d))
        pb = lambda n, s, d: ctx.enter_context(nc.psum_tensor("s_" + n, s, d))
        sem = lambda n: ctx.enter_context(nc.semaphore("s_" + n))
        stage = sb("stage", [P, 2, 2 * C], F32)
        rest = sb("rest", [P, 2, P], F32)
        top = sb("top", [P, 2, P], F32)
        tick = sb("tick", [P, 2], F32)
        S = sb("S", [P, PAIRS, P + 1], F32)
        gap = sb("gap", [P, PAIRS, P], F32)
        resid = sb("resid", [P, PAIRS, P], F32)
        gstage = sb("gstage", [P, 2, 4, P], F32)
        colp = pb("colp", [P, 2, 512], F32)
        gapp = pb("gapp", [P, 2, 4, P], F32)
        gapT = S[:].rearrange("p a q -> p (a q)")[:, 0:PAIRS * P].rearrange("p (a q) -> p a q", q=P)
        staged, turned, work, gstaged, gturned, gkept, split = (
            sem(n) for n in ("staged", "turned", "work", "gstaged", "gturned", "gkept", "split"))
        PER = 2 + 16 * 2 + 15 * 2 + 31 + 2
        block = ctx.enter_context(nc.Block())

        @block.scalar
        def _(act):
            def body(i, first):
                for p in range(2):
                    if not first:
                        act.wait_ge(turned, 2 * i + p - 1)
                    pair = bass.ds(4 * i + 2 * p, 2)
                    act.copy(stage[:, p].rearrange("k (g c) -> k g c", g=2), t.xs[:, pair]).then_inc(staged, 1)
            body(0, True)
            with act.Fori(1, TURNS) as i:
                body(i, False)
            act.wait_ge(split, 7)

            def turn(j, p):
                act.wait_ge(gturned, j + 1)
                act.mul(gapT[:, bass.ds(4 * j, 4)], gapp[:, p], 0.25).then_inc(gkept, 1)
            rounds(act, PAIRS // 4, turn)

        @block.gpsimd
        def _(gp):
            gp.wait_ge(split, 2)

            def turn(j, p):
                at_least(gp, gturned, j - 1)
                gp.tensor_copy(gstage[:, p], gap[:, bass.ds(4 * j, 4)]).then_inc(gstaged, 1)
            for j in range(PAIRS // 4):
                turn(j, j % 2)

        @block.tensor
        def _(pe):
            def body(i, first):
                for p in range(2):
                    pe.wait_ge(staged, 2 * i + p + 1)
                    if not first:
                        pe.wait_ge(work, i * PER - PER + 3)
                    pe.transpose(colp[:, p, 0:P], stage[:, p], t.eye[:]).then_inc(turned, 1)
            body(0, True)
            with pe.Fori(1, TURNS) as i:
                body(i, False)

            def turn(j, p):
                pe.wait_ge(gstaged, j + 1)
                at_least(pe, gkept, j - 1)
                for n in range(4):
                    last = pe.transpose(gapp[:, p, n], gstage[:, p, n], t.eye[:])
                last.then_inc(gturned, 1)
            rounds(pe, PAIRS // 4, turn)

        @block.vector
        def _(dve):
            dve.memset(S[:, :, 0], TOP).then_inc(work, 1)
            with dve.Fori(0, TURNS) as i:
                n = 0

                def count(ins):
                    nonlocal n
                    ins.then_inc(work, 1)
                    n += 1

                def settle():
                    dve.wait_ge(work, i * PER + n + 1)
                    count(dve.memset(tick[:], 0.0))

                dve.wait_ge(work, i * PER + 1)
                dve.wait_ge(turned, 2 * i + 2)
                for p in range(2):
                    count(dve.tensor_copy(rest[:, p], colp[:, p, 0:P]))
                for r in range(16):
                    settle()
                    for p in range(2):
                        count(dve.max(top[:, p, 8 * r:8 * r + 8], rest[:, p]))
                    if r < 15:
                        settle()
                        for p in range(2):
                            count(dve.match_replace(rest[:, p], top[:, p, 8 * r:8 * r + 8], rest[:, p], LOW))
                dve.wait_ge(work, i * PER + n + 1)
                for p in range(2):
                    count(dve.tensor_copy(S[:, bass.ds(2 * i + p, 1), 1:P + 1].rearrange("p o q -> p (o q)"), top[:, p]))
                assert n == PER, n
            dve.wait_ge(work, TURNS * PER + 1)
            link = chain(dve, split, 0)
            link(dve.tensor_tensor(out=gap[:, :, 1:P], in0=S[:, :, 2:P + 1], in1=S[:, :, 1:P], op=ALU.subtract))
            link(dve.tensor_copy(gap[:, :, 0], S[:, :, 1]))
            s = S[:, :, 0:P]
            link(dve.tensor_copy(t.Sparts[:, 0], s))
            link(dve.tensor_tensor(out=resid[:], in0=s, in1=t.Sparts[:, 0], op=ALU.subtract))
            link(dve.tensor_copy(t.Sparts[:, 1], resid[:]))
            link(dve.tensor_tensor(out=resid[:], in0=resid[:], in1=t.Sparts[:, 1], op=ALU.subtract))
            assert link(dve.tensor_copy(t.Sparts[:, 2], resid[:])) == 7
            dve.wait_ge(gkept, PAIRS // 4)
            link(dve.tensor_copy(t.gaps[:, :, :, 0], gapT))
            link(dve.tensor_tensor(out=resid[:], in0=gapT, in1=t.gaps[:, :, :, 0], op=ALU.subtract))
            link(dve.tensor_copy(t.gaps[:, :, :, 1], resid[:]))
            link(dve.tensor_tensor(out=resid[:], in0=resid[:], in1=t.gaps[:, :, :, 1], op=ALU.subtract))
            link(dve.tensor_copy(t.gaps[:, :, :, 2], resid[:]))


SETS = C // 4
TILES = C // 2
CLIP = "AADAADAD"
KIND = [CLIP[n % 8] for n in range(TILES)]
UPTO = {k: [KIND[:n].count(k) for n in range(TILES + 1)] for k in "DA"}
FORDER = sorted(range(TILES), key=lambda n: n + (1.5 if KIND[n] == "A" else 0))
PLACE = [FORDER.index(n) for n in range(TILES)]
FLAG = 3
ABOVE, COPIES, CLIPS = 4, 4, 4


def quantiles(nc, t):
    with ExitStack() as ctx:
        sb = lambda n, s, d: ctx.enter_context(nc.sbuf_tensor("q_" + n, s, d))
        pb = lambda n, s, d: ctx.enter_context(nc.psum_tensor("q_" + n, s, d))
        sem = lambda n: ctx.enter_context(nc.semaphore("q_" + n))
        rows = sb("rows", [32 + 3, 2, 32 * P], BF16)
        left = sb("left", [P, 3, P], BF16)
        base = sb("base", [P, 2, 3, P], BF16)
        nv = sb("nv", [P, 2, P], BF16)
        xg = sb("xg", [P, 2, C], F32)
        gap1, gap2 = sb("gap1", [P, 2, C, 3], BF16), sb("gap2", [P, 2, C, 3], BF16)
        nil = sb("nil", [P, C, 3], BF16)
        above = sb("above", [P, ABOVE, 4, P], BF16)
        copies = sb("copies", [P, COPIES, 2, 3 * P], BF16)
        clips = sb("clips", [P, CLIPS, 2, 3 * P], BF16)
        srow = pb("srow", [P, 2, 4, P], F32)
        cnt = pb("cnt", [P, 2, 2, 512], F32)
        aggp = pb("aggp", [P, 2, 512], F32)
        set_, set_gp, prep, prep_gp, bcast, compared, counted, direct, taken, clipped, reduced, kept = (
            sem(n) for n in ("set", "set_gp", "prep", "prep_gp", "bcast", "compared", "counted", "direct", "taken",
                             "clipped", "reduced", "kept"))
        rows_in = [sem(f"rows_in{p}") for p in range(2)]
        block = ctx.enter_context(nc.Block())

        def pair_loop(eng, body):
            body(0)
            with eng.Fori(1, PAIRS - 1) as i:
                body(i)
            body(PAIRS - 1)

        ends = lambda i, p: isinstance(i, int) and i == PAIRS - 1 and p == 1

        @block.sync
        def _(sp):
            def flatten(i, p):
                g = 2 * i + p
                at_least(sp, bcast, (g - 1) * SETS)
                for s in range(3):
                    for q in range(2):
                        src = t.Sparts[64 * p + 32 * q:64 * p + 32 * q + 32, s, bass.ds(i, 1), :]
                        sp.dma_start(rows[32 * q + s:32 * q + s + 1, p, :].rearrange("o (c k) -> o c k", c=32),
                                     src.rearrange("c o k -> c (o k)")).then_inc(rows_in[p], 16)
            flatten(0, 0)

            def body(i):
                for p in range(2):
                    if not ends(i, p):
                        flatten(i + p, 1 - p)
            pair_loop(sp, body)

        @block.gpsimd
        def _(gp):
            gp.memset(nil[:], 0.0).then_inc(set_gp, 1)
            gp.wait_ge(set_gp, 1)

            def prepare(i, p):
                g = 2 * i + p
                at_least(gp, compared, (g - 1) * SETS)
                at_least(gp, reduced, (g - 1) * TILES)
                gp.tensor_tensor(out=xg[:, p], in0=t.xs[:, bass.ds(g, 1), :].rearrange("p o c -> p (o c)"), in1=nil[:, :, 0],
                                 op=ALU.add).then_inc(prep_gp, 1)
                gaps = t.gaps[:, bass.ds(i, 1), C * p:C * p + C, :].rearrange("p o c s -> p (o c) s")
                gp.tensor_tensor(out=gap1[:, p], in0=gaps, in1=nil[:], op=ALU.add).then_inc(prep_gp, 1)
                gp.tensor_tensor(out=gap2[:, p], in0=gaps, in1=gaps, op=ALU.add).then_inc(prep_gp, 1)
            prepare(0, 0)

            def body(i):
                for p in range(2):
                    if not ends(i, p):
                        prepare(i + p, 1 - p)
            pair_loop(gp, body)

        @block.scalar
        def _(act):
            def body(i):
                for p in range(2):
                    g = 2 * i + p
                    for n in range(TILES):
                        if KIND[n] == "A":
                            a = UPTO["A"][n]
                            act.wait_ge(counted, g * TILES + n + 1)
                            back = a - COPIES
                            if back >= 0:
                                act.wait_ge(clipped, g * TILES + PLACE[KINDA[back]] + 1)
                            else:
                                at_least(act, clipped, (g - 1) * TILES + PLACE[KINDA[back]] + 1)
                            act.copy(copies[:, a % COPIES], cnt[:, n % 2, :, 0:3 * P]).then_inc(taken, 1)
            pair_loop(act, body)

        @block.vector
        def _(dve):
            for n, tau in enumerate(TAUS):
                dve.tensor_scalar(left[:, n], t.eye[:], 1.0 - tau, None, ALU.mult).then_inc(set_, 1)
            dve.wait_ge(set_, 3)

            def prepare(i, p):
                g = 2 * i + p
                at_least(dve, counted, (g - 1) * TILES)
                v = t.negV[:, bass.ds(g, 1), :].rearrange("p o k -> p (o k)")
                dve.tensor_copy(nv[:, p], v).then_inc(prep, 1)
                for n, tau in enumerate(TAUS):
                    dve.scalar_tensor_tensor(out=base[:, p, n], in0=v, scalar=-tau, in1=left[:, n],
                                             op0=ALU.mult, op1=ALU.add).then_inc(prep, 1)

            def compare(g, p, s):
                dve.wait_ge(bcast, g * SETS + s + 1)
                at_least(dve, counted, g * TILES + 2 * (s - ABOVE + 1))
                x = xg[:, p, 4 * s:4 * s + 4].unsqueeze(2).broadcast_to([P, 4, P])
                dve.tensor_tensor(out=above[:, s % ABOVE], in0=srow[:, s % 2], in1=x, op=ALU.is_le).then_inc(compared, 1)

            def keep(g, p):
                dve.wait_ge(reduced, (g + 1) * TILES)
                dve.tensor_reduce(t.agg[:, bass.ds(g, 1), :].rearrange("p o c -> p (o c)"),
                                  aggp[:, p, 0:3 * C].rearrange("p (c s) -> p c s", s=3), AX.X, ALU.add).then_inc(kept, 1)

            prepare(0, 0)

            def body(i):
                for p in range(2):
                    g = 2 * i + p
                    dve.wait_ge(prep_gp, 3 * g + 1)
                    compare(g, p, 0)
                    for m, n in enumerate(FORDER):
                        if m % 2 == 0 and m // 2 + 1 < SETS:
                            compare(g, p, m // 2 + 1)
                        at_least(dve, reduced, g * TILES + m - CLIPS + 1)
                        if KIND[n] == "D":
                            dve.wait_ge(counted, g * TILES + n + 1)
                            src = cnt[:, n % 2, :, 0:3 * P]
                        else:
                            dve.wait_ge(taken, g * UPTO["A"][TILES] + UPTO["A"][n] + 1)
                            src = copies[:, UPTO["A"][n] % COPIES]
                        dve.tensor_scalar(clips[:, m % CLIPS], src, 0.0, 1.0, ALU.max, ALU.min).then_inc(clipped, 1)
                        if m == 8 and not (isinstance(g, int) and g == 0):
                            keep(g - 1, 1 - p)
                        if m == 20 and not ends(i, p):
                            prepare(i + p, 1 - p)
            pair_loop(dve, body)
            keep(B - 1, 1)

        @block.tensor
        def _(pe):
            def broadcast(g, p, s):
                at_least(pe, compared, g * SETS + s - 1)
                q, c = divmod(4 * s, 32)
                pe.matmul(srow[:, s % 2], t.ones[32 * q:32 * q + 3, :], rows[32 * q:32 * q + 3, p, c * P:(c + 4) * P],
                          start=True, stop=True).then_inc(bcast, 1)

            def count(g, p, n):
                s = n // 2
                if n % 2 == 0:
                    pe.wait_ge(compared, g * SETS + s + 1)
                b = n - 2
                if b >= 0:
                    v = g * TILES + PLACE[b] + 1 if KIND[b] == "D" else g * UPTO["A"][TILES] + UPTO["A"][b] + 1
                else:
                    v = (g - 1) * TILES + PLACE[b] + 1 if KIND[b] == "D" else (g - 1) * UPTO["A"][TILES] + UPTO["A"][b + TILES] + 1
                at_least(pe, clipped if KIND[b] == "D" else taken, v)
                for h in range(2):
                    pe.matmul(cnt[:, n % 2, h, 0:3 * P], t.ones[:], base[:, p], start=True, stop=False)
                for h in range(2):
                    last = pe.matmul(cnt[:, n % 2, h, 0:3 * P], above[:, s % ABOVE, 2 * (n % 2) + h],
                                     nv[:, p].unsqueeze(1).broadcast_to([P, 3, P]), start=False, stop=True)
                last.then_inc(counted, 1)

            def reduce(g, p, m):
                n = FORDER[m]
                pe.wait_ge(clipped, g * TILES + m + 1)
                for h in range(2):
                    c = 2 * n + h
                    for k in range(3):
                        last = pe.matmul(aggp[:, p, 3 * c:3 * c + 3], clips[:, m % CLIPS, h, k * P:(k + 1) * P],
                                         (gap2 if k == 1 else gap1)[:, p, c], start=(k == 0), stop=(k == 2))
                last.then_inc(reduced, 1)

            def body(i):
                for p in range(2):
                    g = 2 * i + p
                    pe.wait_ge(rows_in[p], 96 * (i + 1))
                    pe.wait_ge(prep, 4 * (g + 1))
                    broadcast(g, p, 0)
                    at_least(pe, kept, g - 1)
                    pe.wait_ge(prep_gp, 3 * (g + 1))
                    for n in range(TILES + FLAG):
                        if n < TILES:
                            if n % 2 == 0 and n // 2 + 1 < SETS:
                                broadcast(g, p, n // 2 + 1)
                            count(g, p, n)
                        if n >= FLAG:
                            reduce(g, p, n - FLAG)
            pair_loop(pe, body)


KINDA = [n for n in range(TILES) if KIND[n] == "A"]


def quantile_out(nc, t, W1, b1, W2, b2):
    N = 4
    ROUNDS = B // N
    H = P
    with ExitStack() as ctx:
        sb = lambda n, s, d: ctx.enter_context(nc.sbuf_tensor("m_" + n, s, d))
        pb = lambda n, s, d: ctx.enter_context(nc.psum_tensor("m_" + n, s, d))
        sem = lambda n: ctx.enter_context(nc.semaphore("m_" + n))
        w1, b1c, w2, b2b = sb("w1", [P, 2, H], F32), sb("b1c", [H, 1], F32), sb("w2", [H, C], F32), sb("b2b", [P, C], F32)
        square = sb("square", [P, B, C], F32)
        stat, std = sb("stat", [P, 2, B], F32), sb("std", [P, B], F32)
        stage = sb("stage", [P, 2, N, C], F32)
        oT, h = sb("oT", [P, 2, N // 2, P], F32), sb("h", [H, 2, 2, N // 2, P], F32)
        y2 = sb("y2", [P, N, C], F32)
        oTp, hp, yp = pb("oTp", [P, 2, 512], F32), pb("hp", [H, 2, 2, N // 2, P], F32), pb("yp", [P, 2, 512], F32)
        w_in, staged, turned, copied, hidden, rectified, made, added, done, work, ready, rooted, set_w = (
            sem(n) for n in ("w_in", "staged", "turned", "copied", "hidden", "rectified", "made", "added", "done", "work",
                             "ready", "rooted", "set_w"))
        block = ctx.enter_context(nc.Block())

        @block.sync
        def _(sp):
            sp.wait_ge(set_w, 1)
            for q in range(2):
                sp.dma_start(w1[C * q:C * q + C, q], W1).then_inc(w_in, 16)
            for dst, src in ((b1c, b1), (w2, W2), (b2b, b2)):
                sp.dma_start(dst[:], src).then_inc(w_in, 16)

        @block.gpsimd
        def _(gp):
            def body(j, p):
                here = bass.ds(j * N, N)
                at_least(gp, turned, j - 1)
                gp.tensor_tensor(out=stage[:, p], in0=t.xs[:, here], in1=t.agg[:, here], op=ALU.add).then_inc(staged, 1)
            rounds(gp, ROUNDS, body)

        @block.tensor
        def _(pe):
            pe.wait_ge(w_in, 80)

            def second(j, p):
                pe.wait_ge(rectified, j + 1)
                at_least(pe, added, j - 1)
                for g in range(N):
                    last = pe.matmul(yp[:, p, g * C:(g + 1) * C], h[:, p, g % 2, g // 2], w2[:], start=True, stop=True)
                last.then_inc(made, 1)

            def body(j, p):
                pe.wait_ge(staged, j + 1)
                at_least(pe, copied, j - 1)
                for g in range(N // 2):
                    last = pe.transpose(oTp[:, p, g * P:(g + 1) * P], stage[:, p, 2 * g:2 * g + 2].rearrange("p g c -> p (g c)"), t.eye[:])
                last.then_inc(turned, 1)
                pe.wait_ge(copied, j + 1)
                at_least(pe, rectified, j - 1)
                for q in range(2):
                    last = pe.matmul(hp[:, p, q], w1[:, q], oT[:, p], start=True, stop=True)
                last.then_inc(hidden, 1)
                if not (isinstance(j, int) and j == 0):
                    second(j - 1, 1 - p)
            rounds(pe, ROUNDS, body)
            second(ROUNDS - 1, 1)

        @block.scalar
        def _(act):
            act.wait_ge(w_in, 80)

            def body(j, p):
                act.wait_ge(turned, j + 1)
                at_least(act, hidden, j - 1)
                act.copy(oT[:, p].rearrange("p g k -> p (g k)"), oTp[:, p, 0:N // 2 * P]).then_inc(copied, 1)
                act.wait_ge(hidden, j + 1)
                at_least(act, made, j - 1)
                act.activation(h[:, p], hp[:, p], ACT.Relu, bias=b1c[:, 0:1]).then_inc(rectified, 1)
            rounds(act, ROUNDS, body)
            act.wait_ge(ready, 1)
            act.activation(std[:], stat[:, 1, :], ACT.Sqrt).then_inc(rooted, 1)

        @block.vector
        def _(dve):
            dve.memset(w1[:], 0.0).then_inc(set_w, 1)
            dve.wait_ge(w_in, 80)

            def body(j, p):
                here = bass.ds(j * N, N)
                dve.wait_ge(made, j + 1)
                dve.tensor_tensor(out=y2[:], in0=yp[:, p, 0:N * C].rearrange("p (g c) -> p g c", g=N),
                                  in1=b2b[:].unsqueeze(1).broadcast_to([P, N, C]), op=ALU.add).then_inc(added, 1)
                dve.wait_ge(added, j + 1)
                link = chain(dve, done, 2 * j)
                link(dve.tensor_tensor(out=y2[:], in0=y2[:], in1=t.maskf[:, here].unsqueeze(2).broadcast_to([P, N, C]), op=ALU.mult))
                at_least(dve, staged, j + 1)
                link(dve.tensor_tensor(out=t.xs[:, here], in0=t.xs[:, here], in1=y2[:], op=ALU.add))
            rounds(dve, ROUNDS, body)
            layer_norm(dve, chain(dve, work, 0), t.xs, square, stat, std, ready, rooted, 1)


def gru(nc, t, W1, b1, W2, b2, Wih, bih, Whh, bhh):
    N = 4
    ROUNDS = B // N
    with ExitStack() as ctx:
        sb = lambda n, s, d: ctx.enter_context(nc.sbuf_tensor("g_" + n, s, d))
        pb = lambda n, s, d: ctx.enter_context(nc.psum_tensor("g_" + n, s, d))
        sem = lambda n: ctx.enter_context(nc.semaphore("g_" + n))
        w1, b1c, w2, b2b = sb("w1", [P, 2, C], F32), sb("b1c", [P, 1], F32), sb("w2", [P, 2, C], F32), sb("b2b", [P, C], F32)
        wi, wh = sb("wi", [P, 2, 4, C], F32), sb("wh", [P, 2, 4, C], F32)
        bi, bh, bias = sb("bi", [P, 3, C], F32), sb("bh", [P, 3, C], F32), sb("bias", [P, 4, C], F32)
        square = sb("square", [P, B, C], F32)
        stat, std = sb("stat", [P, 2, B], F32), sb("std", [P, B], F32)
        stage = sb("stage", [P, 2, N, C], F32)
        nil = sb("nil", [P, N, C], F32)
        xT, mT, msgT = sb("xT", [P, 2, N // 2, P], F32), sb("mT", [P, N // 2, P], F32), sb("msgT", [P, N // 2, P], F32)
        m = sb("m", [P, N, C], F32)
        gates, th = sb("gates", [P, 2, N, 4, C], F32), sb("th", [P, 2, N, 2, C], F32)
        new = sb("new", [P, 2, N, C], F32)
        tanh_new = sb("tanh_new", [P, 2, N, C], F32)
        xTp, m1p, m2p, msgp = pb("xTp", [P, 512], F32), pb("m1p", [P, 512], F32), pb("m2p", [P, 512], F32), pb("msgp", [P, N // 2, 2, P], F32)
        gp_ = pb("gatesp", [P, 2, N, 4 * C], F32)
        (w_in, set_, set_gp, staged, turned, copied, made1, act1, made2, biased, act2, made3, act3, made4, gated, work,
         thalf, mixed, tnew, done, ready, rooted, lnwork, set_w) = (
            sem(n) for n in ("w_in", "set", "set_gp", "staged", "turned", "copied", "made1", "act1", "made2", "biased", "act2",
                             "made3", "act3", "made4", "gated", "work", "thalf", "mixed", "tnew", "done", "ready", "rooted", "lnwork", "set_w"))
        block = ctx.enter_context(nc.Block())

        @block.sync
        def _(sp):
            sp.wait_ge(set_w, 4)
            for q in range(2):
                at = slice(C * q, C * q + C)
                for dst, src in ((w1[at, q], W1), (b1c[at], b1), (w2[at, q], W2), (wi[at, q, 0:3], Wih),
                                 (wh[at, q, 0:2], Whh[:, 0:2]), (wh[at, q, 3], Whh[:, 2])):
                    sp.dma_start(dst, src).then_inc(w_in, 16)
            for dst, src in ((b2b, b2), (bi, bih), (bh, bhh)):
                sp.dma_start(dst[:], src).then_inc(w_in, 16)

        @block.gpsimd
        def _(gp):
            gp.memset(nil[:], 0.0).then_inc(set_gp, 1)
            gp.wait_ge(set_gp, 1)

            def body(j, p):
                at_least(gp, turned, j - 1)
                gp.tensor_tensor(out=stage[:, p], in0=t.xs[:, bass.ds(j * N, N)], in1=nil[:], op=ALU.add).then_inc(staged, 1)
            rounds(gp, ROUNDS, body)

        @block.tensor
        def _(pe):
            pe.wait_ge(w_in, 240)
            
            def gates_of(j, p):
                pe.wait_ge(act3, 2 * (j + 1))
                at_least(pe, gated, j - 1)
                for g in range(N // 2):
                    pe.matmul(gp_[:, p, 2 * g:2 * g + 2], msgT[:, g], wi[:].rearrange("p q a c -> p (q a c)"), start=True, stop=False)
                    last = pe.matmul(gp_[:, p, 2 * g:2 * g + 2], xT[:, p, g], wh[:].rearrange("p q a c -> p (q a c)"), start=False, stop=True)
                last.then_inc(made4, 1)

            def body(j, p):
                pe.wait_ge(staged, j + 1)
                at_least(pe, copied, j)
                for g in range(N // 2):
                    last = pe.transpose(xTp[:, g * P:(g + 1) * P], stage[:, p, 2 * g:2 * g + 2].rearrange("p g c -> p (g c)"), t.eye[:])
                last.then_inc(turned, 1)
                pe.wait_ge(copied, j + 1)
                at_least(pe, act1, j)
                pe.matmul(m1p[:, 0:N // 2 * P], w1[:], xT[:, p], start=True, stop=True).then_inc(made1, 1)
                pe.wait_ge(act1, j + 1)
                at_least(pe, biased, j)
                for g in range(N // 2):
                    last = pe.matmul(m2p[:, g * P:(g + 1) * P], mT[:, g], w2[:], start=True, stop=True)
                last.then_inc(made2, 1)
                pe.wait_ge(act2, j + 1)
                at_least(pe, act3, 2 * j)
                for g in range(N // 2):
                    last = pe.matmul(msgp[:, g], m[:, 2 * g:2 * g + 2].rearrange("p g c -> p (g c)"),
                                     t.adjT[:, bass.ds(j * N + 2 * g, 2), :], start=True, stop=True)
                last.then_inc(made3, 1)
                gates_of(j, p)
            rounds(pe, ROUNDS, body)

        @block.scalar
        def _(act):
            act.wait_ge(w_in, 240)

            def body(j, p):
                act.wait_ge(turned, j + 1)
                at_least(act, made4, j - 1)
                act.activation(xT[:, p].rearrange("p g k -> p (g k)"), xTp[:, 0:N // 2 * P], ACT.Copy).then_inc(copied, 1)
                act.wait_ge(made1, j + 1)
                at_least(act, made2, j)
                act.activation(mT[:].rearrange("p g k -> p (g k)"), m1p[:, 0:N // 2 * P], ACT.Relu, bias=b1c[:, 0:1]).then_inc(act1, 1)
                act.wait_ge(made3, j + 1)
                at_least(act, made4, j)
                for q in range(2):
                    act.activation(msgT[C * q:C * q + C], msgp[C * q:C * q + C, :, q], ACT.Relu).then_inc(act3, 1)
                act.wait_ge(gated, j + 1)
                at_least(act, done, 6 * (j - 1))
                act.activation(th[:, p], gates[:, p, :, 0:2], ACT.Tanh, scale=0.5).then_inc(thalf, 1)
                act.wait_ge(mixed, j + 1)
                act.activation(tanh_new[:, p], new[:, p], ACT.Tanh).then_inc(tnew, 1)
            rounds(act, ROUNDS, body)
            act.wait_ge(ready, 1)
            act.activation(std[:], stat[:, 1, :], ACT.Sqrt).then_inc(rooted, 1)

        @block.vector
        def _(dve):
            for w in (w1, w2, wi, wh):
                dve.memset(w[:], 0.0).then_inc(set_w, 1)
            dve.wait_ge(w_in, 240)
            dve.tensor_tensor(out=bias[:, 0:2], in0=bi[:, 0:2], in1=bh[:, 0:2], op=ALU.add).then_inc(set_, 1)
            dve.tensor_copy(bias[:, 2], bi[:, 2]).then_inc(set_, 1)
            dve.tensor_copy(bias[:, 3], bh[:, 2]).then_inc(set_, 1)
            dve.wait_ge(set_, 3)

            def body(j, p):
                here = bass.ds(j * N, N)
                dve.wait_ge(made2, j + 1)
                at_least(dve, made3, j)
                dve.tensor_tensor(out=m[:], in0=m2p[:, 0:N * C].rearrange("p (g c) -> p g c", g=N),
                                  in1=b2b[:].unsqueeze(1).broadcast_to([P, N, C]), op=ALU.add).then_inc(biased, 1)
                dve.wait_ge(biased, j + 1)
                dve.tensor_scalar(m[:], m[:], 0.0, None, ALU.max).then_inc(act2, 1)
                dve.wait_ge(made4, j + 1)
                dve.tensor_tensor(out=gates[:, p].rearrange("p g a c -> p g (a c)"), in0=gp_[:, p],
                                  in1=bias[:].rearrange("p a c -> p (a c)").unsqueeze(1).broadcast_to([P, N, 4 * C]),
                                  op=ALU.add).then_inc(gated, 1)
                link = chain(dve, done, 6 * j)
                dve.wait_ge(thalf, j + 1)
                sig, hn = th[:, p], gates[:, p, :, 3]
                link(dve.tensor_scalar(sig, sig, 0.5, 0.5, ALU.mult, ALU.add))
                link(dve.tensor_tensor(out=new[:, p], in0=sig[:, :, 0], in1=hn, op=ALU.mult))
                dve.tensor_tensor(out=new[:, p], in0=new[:, p], in1=gates[:, p, :, 2], op=ALU.add).then_inc(mixed, 1)
                dve.wait_ge(tnew, j + 1)
                h, n = t.xs[:, here], tanh_new[:, p]
                link(dve.tensor_tensor(out=new[:, p], in0=h, in1=n, op=ALU.subtract))
                link(dve.tensor_tensor(out=new[:, p], in0=new[:, p], in1=sig[:, :, 1], op=ALU.mult))
                link(dve.tensor_tensor(out=new[:, p], in0=new[:, p], in1=n, op=ALU.add))
                dve.wait_ge(staged, j + 1)
                link(dve.tensor_tensor(out=t.xs[:, here], in0=h, in1=new[:, p], op=ALU.add))
            rounds(dve, ROUNDS, body)
            layer_norm(dve, chain(dve, lnwork, 0), t.xs, square, stat, std, ready, rooted, 1)


def build(nc, d, out, stop=9):
    with ExitStack() as ctx:
        sb = lambda n, s, dt: ctx.enter_context(nc.sbuf_tensor(n, s, dt))

        class t:
            xs = sb("xs", [P, B, C], F32)
            adjT = sb("adjT", [P, B, P], F32)
            negV = sb("negV", [P, B, P], BF16)
            rowsum, degree, maskf = (sb(n, [P, B], F32) for n in ("rowsum", "degree", "maskf"))
            eye, onesf = sb("eye", [P, P], F32), sb("onesf", [P, P], F32)
            eyeb, ones = sb("eyeb", [P, P], BF16), sb("ones", [P, P], BF16)

        neighbours(nc, t, d["adj"], d["adjT"], d["mask"], d["x"], d["ident"])
        with nc.sbuf_tensor("hm", [P, B, HID], F32) as hm:
            t.hm = hm
            edge_mlp(nc, t, d["xT"], d["W1"], d["b1"])
            edge_out(nc, t, d["W2"], d["b2"])
        graph_conv(nc, t, d["W_1"], d["gamma"], d["beta"], d["b_1"])
        with nc.sbuf_tensor("Sparts", [P, 3, PAIRS, P], BF16) as Sparts, nc.sbuf_tensor("gaps", [P, PAIRS, P, 3], BF16) as gaps:
            t.Sparts, t.gaps = Sparts, gaps
            sort_columns(nc, t)
            with nc.sbuf_tensor("agg", [P, B, C], F32) as agg:
                t.agg = agg
                quantiles(nc, t)
                quantile_out(nc, t, *(d["2" + n] for n in ("W1", "b1", "W2", "b2")))
        gru(nc, t, *(d["3" + n] for n in ("W1", "b1", "W2", "b2", "W_ih", "b_ih", "W_hh", "b_hh")))
        store(nc, t, out)


def store(nc, t, out):
    with nc.semaphore("stored") as stored, nc.Block() as block:
        @block.sync
        def _(sp):
            sp.dma_start(out, t.xs[:]).then_inc(stored, 16)
            sp.wait_ge(stored, 16)


def kernel(**inputs):
    import numpy as np
    import concourse.bacc as bacc
    from concourse.bass_utils import run_bass_kernel_spmd

    nc = bacc.Bacc("TRN2", target_bir_lowering=False, num_devices=1)
    a = {k: np.asarray(v) for k, v in inputs.items()}
    lay = lambda v: np.ascontiguousarray(v)
    col = lambda n: lay(a[n].reshape(-1, 1))
    vec = lambda n: lay(a[n].reshape(1, -1))
    host = {
        "x": lay(a["x"].transpose(1, 0, 2)),
        "xT": lay(a["x"].transpose(2, 0, 1).reshape(C, B * P)),
        "adj": lay(a["adj"].transpose(1, 0, 2)),
        "adjT": lay(a["adj"].transpose(2, 0, 1)),
        "mask": lay(a["nodemask"].T.view(np.uint8)),
        "ident": np.eye(P, dtype=np.float32),
        "W1": lay(a["L0_gnn_W1"].reshape(2, C, HID).transpose(1, 0, 2)),
        "b1": vec("L0_gnn_b1"),
        "W2": lay(a["L0_gnn_W2"]),
        "b2": vec("L0_gnn_b2"),
        "W_1": lay(a["L1_gnn_W"]), "gamma": vec("L1_gnn_gamma"), "beta": vec("L1_gnn_beta"), "b_1": vec("L1_gnn_b"),
        "2W1": lay(a["L2_gnn_W1"]), "2b1": col("L2_gnn_b1"), "2W2": lay(a["L2_gnn_W2"]), "2b2": vec("L2_gnn_b2"),
        "3W1": lay(a["L3_gnn_W1"]), "3b1": col("L3_gnn_b1"), "3W2": lay(a["L3_gnn_W2"]), "3b2": vec("L3_gnn_b2"),
        "3W_ih": lay(a["L3_gnn_W_ih"].T.reshape(C, 3, C)), "3b_ih": lay(a["L3_gnn_b_ih"].reshape(1, 3, C)),
        "3W_hh": lay(a["L3_gnn_W_hh"].T.reshape(C, 3, C)), "3b_hh": lay(a["L3_gnn_b_hh"].reshape(1, 3, C)),
    }
    d = {n: nc.dram_tensor("in_" + n, v.shape, mybir.dt.from_np(v.dtype), kind="ExternalInput").ap() for n, v in host.items()}
    out = nc.dram_tensor("out", (P, B, C), F32, kind="ExternalOutput").ap()
    for n in ("b2", "gamma", "beta", "b_1", "2b2", "3b2", "3b_ih", "3b_hh"):
        d[n] = d[n].broadcast_to([P, *d[n].shape[1:]])
    build(nc, d, out)
    r = run_bass_kernel_spmd(nc, [{"in_" + n: v for n, v in host.items()}], core_ids=[0])
    return lay(r.results[0]["out"].transpose(1, 0, 2))
```

```python
from contextlib import ExitStack

import concourse.bass as bass
from concourse import mybir

F32, F16, BF16, U8 = mybir.dt.float32, mybir.dt.float16, mybir.dt.bfloat16, mybir.dt.uint8
ALU, ACT, AX = mybir.AluOpType, mybir.ActivationFunctionType, mybir.AxisListType

P = 128
B = 64
C = 64
HID = 192
PAIRS = B // 2
EPS = 1e-5
TAUS = (0.25, 0.5, 0.75)
HUGE = 2.0 ** 126
TOP = 2.0 ** 127


def chain(eng, sem, start):
    n = [0]

    def link(ins):
        ins.then_inc(sem, 1)
        n[0] += 1
        eng.wait_ge(sem, start + n[0])
        return n[0]
    return link


def layer_norm(dve, link, xs, square, stat, std, ready, rooted, roots):
    wide = lambda v: v.unsqueeze(2).broadcast_to([P, B, C])
    link(dve.tensor_reduce(stat[:, 0, :], xs[:], AX.X, ALU.add))
    link(dve.tensor_scalar(stat[:, 0, :], stat[:, 0, :], 1.0 / C, None, ALU.mult))
    link(dve.tensor_tensor(out=xs[:], in0=xs[:], in1=wide(stat[:, 0, :]), op=ALU.subtract))
    link(dve.tensor_tensor(out=square[:], in0=xs[:], in1=xs[:], op=ALU.mult))
    link(dve.tensor_reduce(stat[:, 0, :], square[:], AX.X, ALU.add))
    dve.tensor_scalar(stat[:, 1, :], stat[:, 0, :], 1.0 / C, EPS, ALU.mult, ALU.add).then_inc(ready, 1)
    dve.wait_ge(rooted, roots)
    link(dve.reciprocal(stat[:, 0, :], std[:]))
    link(dve.tensor_tensor(out=xs[:], in0=xs[:], in1=wide(stat[:, 0, :]), op=ALU.mult))


def neighbours(nc, t, adj, adjT, mask, x, ident):
    G = 8
    CH = B // G
    with ExitStack() as ctx:
        sb = lambda n, s, d: ctx.enter_context(nc.sbuf_tensor(n, s, d))
        pb = lambda n, s, d: ctx.enter_context(nc.psum_tensor(n, s, d))
        sem = lambda n: ctx.enter_context(nc.semaphore(n))
        adjc = sb("adjc", [P, 2, G, P], F32)
        running = sb("running", [P, G, P], F32)
        pos, nb, rank, t1, first, both = (sb(n, [P, G, P], BF16) for n in ("pos", "nb", "rank", "t1", "first", "both"))
        zero = sb("zero", [P, G * P], F32)
        basis = sb("basis", [P, G], F32)
        count = sb("count", [P, G], F32)
        m, even, cut = (sb(n, [P, G], BF16) for n in ("m", "even", "cut"))
        rem, sym, a1 = (sb(n, [P, G, P], BF16) for n in ("rem", "sym", "a1"))
        noteye = sb("noteye", [P, P], BF16)
        mask8 = sb("mask8", [P, B], U8)
        remT = pb("remT", [P, G, P], BF16)
        loaded, work, turned = sem("n_loaded"), sem("n_work"), sem("n_turned")
        chunk_in = [sem("n_chunk_in0"), sem("n_chunk_in1")]
        OPS, SETUP, REM_AT = 22, 12, 19
        block = ctx.enter_context(nc.Block())

        @block.sync
        def _(sp):
            sp.dma_start(t.eye[:], ident).then_inc(loaded, 16)
            sp.dma_start(mask8[:], mask).then_inc(loaded, 16)
            sp.dma_start(adjc[:, 0], adj[:, 0:G]).then_inc(chunk_in[0], 16)
            sp.dma_start(adjc[:, 1], adj[:, G:2 * G]).then_inc(chunk_in[1], 16)
            sp.dma_start(t.xs[:], x).then_inc(loaded, 16)
            sp.dma_start(t.adjT[:], adjT).then_inc(loaded, 16)
            with sp.Fori(1, CH // 2) as i:
                for p in range(2):
                    sp.wait_ge(work, SETUP + (2 * i + p - 2) * OPS + OPS)
                    sp.dma_start(adjc[:, p], adj[:, bass.ds((2 * i + p) * G, G)]).then_inc(chunk_in[p], 16)

        @block.vector
        def _(dve):
            link = chain(dve, work, 0)
            link(dve.memset(zero[:], 0.0))
            link(dve.memset(basis[:], 0.0))
            link(dve.memset(t.ones[:], 1.0))
            link(dve.memset(t.onesf[:], 1.0))
            link(dve.memset(t.pick[:], 0.0))
            for q in range(4):
                link(dve.memset(t.pick[32 * q:32 * q + 3, q], 1.0))
            dve.wait_ge(loaded, 64)
            link(dve.tensor_copy(t.maskf[:], mask8[:]))
            link(dve.tensor_copy(t.eyeb[:], t.eye[:]))
            assert link(dve.tensor_scalar(noteye[:], t.eye[:], -1.0, 1.0, ALU.mult, ALU.add)) == SETUP
            wide = lambda v: v.unsqueeze(2).broadcast_to([P, G, P])
            over = lambda v: v.unsqueeze(1).broadcast_to([P, G, P])
            with dve.Fori(0, CH // 2) as i:
                for p in range(2):
                    j = 2 * i + p
                    here = bass.ds(j * G, G)
                    link = chain(dve, work, SETUP + j * OPS)
                    dve.wait_ge(chunk_in[p], 16 * (i + 1))
                    link(dve.tensor_reduce(t.rowsum[:, here], adjc[:, p], AX.X, ALU.add))
                    link(dve.tensor_scalar(pos[:], adjc[:, p], 0.0, None, ALU.is_gt))
                    link(dve.tensor_reduce(t.degree[:, here], pos[:], AX.X, ALU.add))
                    link(dve.tensor_tensor(out=nb[:], in0=pos[:], in1=over(noteye[:]), op=ALU.mult))
                    link(dve.tensor_reduce(count[:], nb[:], AX.X, ALU.add))
                    link(dve.tensor_copy(m[:], count[:]))
                    link(dve.tensor_tensor_scan(running[:].rearrange("p g k -> p (g k)"), nb[:].rearrange("p g k -> p (g k)"),
                                                zero[:], 0.0, ALU.add, ALU.add))
                    link(dve.tensor_copy(basis[:, 1:G], running[:, 0:G - 1, P - 1]))
                    link(dve.tensor_tensor(out=rank[:], in0=running[:], in1=wide(basis[:]), op=ALU.subtract))
                    link(dve.scalar_tensor_tensor(out=t1[:], in0=rank[:], scalar=2.0, in1=wide(m[:]), op0=ALU.mult, op1=ALU.subtract))
                    link(dve.scalar_tensor_tensor(out=first[:], in0=t1[:], scalar=0.0, in1=nb[:], op0=ALU.is_equal, op1=ALU.mult))
                    link(dve.tensor_reduce(even[:], first[:], AX.X, ALU.max))
                    link(dve.scalar_tensor_tensor(out=both[:], in0=t1[:], scalar=1.0, in1=first[:], op0=ALU.is_equal, op1=ALU.add))
                    link(dve.tensor_tensor(out=t1[:], in0=rank[:], in1=wide(m[:]), op=ALU.is_equal))
                    link(dve.tensor_tensor(out=t1[:], in0=t1[:], in1=wide(even[:]), op=ALU.mult))
                    link(dve.tensor_tensor(out=both[:], in0=both[:], in1=t1[:], op=ALU.add))
                    link(dve.scalar_tensor_tensor(out=cut[:], in0=m[:], scalar=10.0, in1=t.maskf[:, here], op0=ALU.is_gt, op1=ALU.mult))
                    link(dve.tensor_tensor(out=both[:], in0=both[:], in1=nb[:], op=ALU.mult))
                    assert link(dve.tensor_tensor(out=rem[:], in0=both[:], in1=wide(cut[:]), op=ALU.mult)) == REM_AT
                    link(dve.scalar_tensor_tensor(out=a1[:], in0=t.adjT[:, here], scalar=0.0, in1=over(t.eye[:]), op0=ALU.is_gt, op1=ALU.max))
                    dve.wait_ge(turned, j + 1)
                    link(dve.tensor_tensor(out=sym[:], in0=rem[:], in1=remT[:], op=ALU.max))
                    assert link(dve.scalar_tensor_tensor(out=t.negV[:, here], in0=sym[:], scalar=1.0, in1=a1[:],
                                                         op0=ALU.subtract, op1=ALU.mult)) == OPS

        @block.tensor
        def _(pe):
            with pe.Fori(0, CH) as j:
                pe.wait_ge(work, SETUP + j * OPS + REM_AT)
                for g in range(G):
                    last = pe.transpose(remT[:, g], rem[:, g], t.eyeb[:])
                last.then_inc(turned, 1)


BANKS = HID // 4
KINDS = "DADADDADADADDADA"
DONE = {k: [sum(KINDS[b % 16] == k for b in range(n)) for n in range(BANKS + 1)] for k in "DA"}
A_LAG = 3
PROJECT_AT = (9, 17, 25)
SPAN = HID // 4
ORDER = sorted(range(BANKS), key=lambda b: b + (A_LAG + 0.5 if KINDS[b % 16] == "A" else 0))
RING, CMPS, SIGNS = 6, 12, 7
RED_LAG = 8


def edge_mlp(nc, t, xT, W1, b1):
    with ExitStack() as ctx:
        sb = lambda n, s, d: ctx.enter_context(nc.sbuf_tensor(n, s, d))
        pb = lambda n, s, d: ctx.enter_context(nc.psum_tensor(n, s, d))
        sem = lambda n: ctx.enter_context(nc.semaphore(n))
        w1 = sb("w1", [C, 2, HID], F32)
        wuv = sb("wuv", [C + 1, 2 * HID], F32)
        xTg = sb("xTg", [C + 1, 2, P], F32)
        uv = sb("uv", [P, 2, 2 * HID], F32)
        negv = sb("negv", [P, 2, HID], F32)
        uT = sb("uT", [P, 2, P], F32)
        uTparts = sb("uTparts", [P, 2, 3, 2, P], BF16)
        ru = sb("ru", [P, 2, P], F32)
        rv = sb("rv", [P, HID], F32)
        one_v = sb("one_v", [P, 2, HID, 4], BF16)
        rows = sb("rows", [P, 2, SPAN * P], BF16)
        far = sb("far", [P, 2, P], BF16)
        away = sb("away", [P, 2, P], BF16)
        signs = sb("signs", [P, SIGNS, 4, P], BF16)
        cmps = sb("cmps", [P, CMPS, 4, P], BF16)
        sums = sb("sums", [P, HID, 4], F32)
        part = sb("part", [P, HID], F32)
        nil = sb("nil", [P, 2, P], F32)
        nil_v = nil[:].rearrange("p a k -> p (a k)")[:, 0:HID]
        bank = pb("bank", [P, RING, 4, P], F32)
        sums_scratch = pb("sums_scratch", [P, 1024], F32)
        red = sums_scratch[:, 0:4 * HID].rearrange("p (h s) -> p h s", s=4)
        scratch = sums_scratch[:, 4 * HID:1024]
        w_in, set_, uv_ps, uv_sb, pool = (sem("e_" + n) for n in ("w_in", "set", "uv_ps", "uv_sb", "pool"))
        x_in, rows_in = ([sem(f"e_{n}{p}") for p in range(2)] for n in ("x_in", "rows_in"))
        masked, bcast, compared, signed, cmp_done, reduced, sums_done, set_act = (
            sem("e_" + n) for n in ("masked", "bcast", "compared", "signed", "cmp_done", "reduced", "sums_done", "set_act"))
        set_gp = sem("e_set_gp")
        POOL = 14
        block = ctx.enter_context(nc.Block())

        def pair_loop(eng, body):
            body(0)
            with eng.Fori(1, PAIRS - 1) as i:
                body(i)
            body(PAIRS - 1)

        def after(eng, sem_, g, per, n):
            v = g * per + n
            if not isinstance(v, int) or v > 0:
                eng.wait_ge(sem_, v)

        RUNS = [(0, 48), (48, 48), (96, 32), (128, 16), (144, 48)]
        ROWS_IN = 16 * 3 * len(RUNS)

        @block.sync
        def _(sp):
            sp.dma_start(w1[:], W1).then_inc(w_in, 16)
            sp.dma_start(wuv[C:C + 1, 0:HID], b1).then_inc(w_in, 16)

            def load(i, p):
                g = 2 * i + p
                after(sp, uv_ps, g - 2, 3, 3)
                sp.dma_start(xTg[0:C, p], xT[:, bass.ds(g * P, P)]).then_inc(x_in[p], 16)

            def flatten(i, p):
                g = 2 * i + p
                sp.wait_ge(pool, g * POOL + 5)
                after(sp, bcast, g - 2, BANKS, BANKS)
                for s in range(3):
                    for h, n in RUNS:
                        q, c = divmod(h, SPAN)
                        sp.dma_start(rows[32 * q + s:32 * q + s + 1, p, c * P:(c + n) * P].rearrange("o (h k) -> o h k", h=n),
                                     uTparts[h % P:h % P + n, p, s, h // P, :]).then_inc(rows_in[p], 16)

            load(0, 0)
            load(0, 1)
            sp.wait_ge(set_, 5)
            flatten(0, 0)

            def body(i):
                for p in range(2):
                    g = 2 * i + p
                    last = isinstance(i, int) and i == PAIRS - 1
                    if not (last):
                        load(i + 1, p)
                    if not (last and p == 1):
                        flatten(i + p, 1 - p)
            pair_loop(sp, body)

        @block.gpsimd
        def _(gp):
            gp.memset(one_v[:], 1.0).then_inc(set_gp, 1)
            gp.wait_ge(set_gp, 1)
            gp.memset(uT[64:P, 1, :], 0.0).then_inc(set_gp, 1)
            gp.wait_ge(set_gp, 2)
            gp.memset(nil[:], 0.0).then_inc(set_gp, 1)
            gp.wait_ge(set_gp, 3)

            def parts(i, p):
                g = 2 * i + p
                link = chain(gp, pool, g * POOL)
                gp.wait_ge(uv_sb, 4 * g + 2)
                after(gp, rows_in[p], i, ROWS_IN, 0)
                link(gp.tensor_tensor(out=uTparts[:, p, 0], in0=uT[:], in1=nil[:], op=ALU.add))
                link(gp.tensor_tensor(out=ru[:], in0=uT[:], in1=uTparts[:, p, 0], op=ALU.subtract))
                link(gp.tensor_tensor(out=uTparts[:, p, 1], in0=ru[:], in1=nil[:], op=ALU.add))
                link(gp.tensor_tensor(out=ru[:], in0=ru[:], in1=uTparts[:, p, 1], op=ALU.subtract))
                link(gp.tensor_tensor(out=uTparts[:, p, 2], in0=ru[:], in1=nil[:], op=ALU.add))
                after(gp, reduced, g - 2, BANKS, BANKS)
                gp.wait_ge(uv_sb, 4 * g + 3)
                v = uv[:, p, HID:2 * HID]
                link(gp.tensor_tensor(out=one_v[:, p, :, 1], in0=v, in1=nil_v, op=ALU.add))
                link(gp.tensor_tensor(out=rv[:], in0=v, in1=one_v[:, p, :, 1], op=ALU.subtract))
                link(gp.tensor_tensor(out=one_v[:, p, :, 2], in0=rv[:], in1=nil_v, op=ALU.add))
                link(gp.tensor_tensor(out=rv[:], in0=rv[:], in1=one_v[:, p, :, 2], op=ALU.subtract))
                link(gp.tensor_tensor(out=one_v[:, p, :, 3], in0=rv[:], in1=nil_v, op=ALU.add))

            def finish(g, p):
                link = chain(gp, pool, (g + 1) * POOL + (10 if not (isinstance(g, int) and g == B - 1) else 0))
                gp.wait_ge(sums_done, g + 1)
                gp.wait_ge(uv_sb, 4 * g + 4)
                link(gp.tensor_tensor(out=part[:], in0=sums[:, :, 3], in1=sums[:, :, 2], op=ALU.add))
                link(gp.tensor_tensor(out=part[:], in0=part[:], in1=sums[:, :, 1], op=ALU.add))
                link(gp.tensor_tensor(out=rv[:], in0=sums[:, :, 0], in1=uv[:, p, 0:HID], op=ALU.mult))
                link(gp.tensor_tensor(out=t.hm[:, bass.ds(g, 1), :].rearrange("p o h -> p (o h)"), in0=rv[:], in1=part[:], op=ALU.subtract))

            parts(0, 0)
            gp.memset(part[:], 0.0).then_inc(pool, 4)
            gp.wait_ge(pool, POOL)

            def body(i):
                for p in range(2):
                    g = 2 * i + p
                    if not (isinstance(i, int) and i == PAIRS - 1 and p == 1):
                        parts(i + p, 1 - p)
                    finish(g, p)
            pair_loop(gp, body)

        @block.scalar
        def _(act):
            def spread(i, p, k):
                g = 2 * i + p
                act.wait_ge(uv_ps, 3 * g + k + 1)
                if k == 0:
                    after(act, pool, g, POOL, 0)
                    act.copy(uT[:, 0], scratch[:, 0:P]).then_inc(uv_sb, 1)
                    act.copy(uT[0:64, 1], scratch[0:64, P:2 * P]).then_inc(uv_sb, 1)
                if k == 1:
                    after(act, compared, g - 2, DONE["D"][BANKS], DONE["D"][BANKS])
                    after(act, signed, g - 2, DONE["A"][BANKS], DONE["A"][BANKS])
                    act.mul(negv[:, p], scratch[:, 0:HID], -1.0).then_inc(set_act, 1)
                    act.copy(uv[:, p, HID:2 * HID], scratch[:, 0:HID]).then_inc(uv_sb, 1)
                if k == 2:
                    act.copy(uv[:, p, 0:HID], scratch[:, 0:HID]).then_inc(uv_sb, 1)

            def take_sums(g):
                act.wait_ge(reduced, (g + 1) * BANKS)
                after(act, pool, g, POOL, POOL)
                act.copy(sums[:], red).then_inc(sums_done, 1)

            TAKE_AT = next(b for b in range(RED_LAG, BANKS) if KINDS[b % 16] == "A")
            SPREAD_AT = [next(b for b in range(at + 1, BANKS) if KINDS[b % 16] == "A") for at in PROJECT_AT]
            act.wait_ge(set_gp, 3)
            for k in range(3):
                spread(0, 0, k)

            def body(i):
                for p in range(2):
                    g = 2 * i + p
                    act.wait_ge(set_act, g + 1)
                    for b in range(BANKS):
                        if KINDS[b % 16] == "D":
                            continue
                        if b == TAKE_AT and not (isinstance(g, int) and g == 0):
                            take_sums(g - 1)
                        n = DONE["A"][b]
                        act.wait_ge(bcast, g * BANKS + b + 1)
                        after(act, cmp_done, g, DONE["A"][BANKS], n - SIGNS + 1)
                        for h in range(4):
                            ins = act.activation(signs[:, n % SIGNS, h], bank[:, b % RING, h], ACT.Sign,
                                                 bias=negv[:, p, 4 * b + h:4 * b + h + 1])
                        ins.then_inc(signed, 1)
                        if b in SPREAD_AT and not (isinstance(i, int) and i == PAIRS - 1 and p == 1):
                            spread(i + p, 1 - p, SPREAD_AT.index(b))
            pair_loop(act, body)
            take_sums(B - 1)

        @block.vector
        def _(dve):
            dve.wait_ge(w_in, 32)
            dve.tensor_tensor(out=wuv[0:C, 0:HID], in0=w1[:, 0], in1=w1[:, 1], op=ALU.add).then_inc(set_, 1)
            dve.tensor_copy(wuv[0:C, HID:2 * HID], w1[:, 1]).then_inc(set_, 1)
            dve.memset(wuv[C:C + 1, HID:2 * HID], 0.0).then_inc(set_, 1)
            dve.memset(xTg[C:C + 1], 1.0).then_inc(set_, 1)
            dve.memset(rows[:], 0.0).then_inc(set_, 1)

            def masks(i, p):
                g = 2 * i + p
                after(dve, bcast, g - 2, BANKS, BANKS)
                after(dve, cmp_done, g - 2, DONE["A"][BANKS], DONE["A"][BANKS])
                a = t.adjT[:, bass.ds(g, 1), :].rearrange("p o k -> p (o k)")
                dve.tensor_scalar(away[:, p], a, 0.0, -HUGE, ALU.is_le, ALU.mult).then_inc(masked, 1)
                dve.tensor_scalar(far[:, p], a, 0.0, None, ALU.is_le).then_inc(masked, 1)

            masks(0, 0)

            def body(i):
                for p in range(2):
                    g = 2 * i + p
                    dve.wait_ge(uv_sb, 4 * g + 3)
                    dve.wait_ge(masked, 2 * (g + 1))
                    for n, b in enumerate(ORDER):
                        cmp = cmps[:, n % CMPS]
                        after(dve, reduced, g, BANKS, n - CMPS + 1)
                        if KINDS[b % 16] == "D":
                            dve.wait_ge(bcast, g * BANKS + b + 1)
                            v = uv[:, p, HID + 4 * b:HID + 4 * b + 4].unsqueeze(2).broadcast_to([P, 4, P])
                            ins = dve.tensor_tensor(out=cmp, in0=bank[:, b % RING], in1=v, op=ALU.is_gt)
                            ins.then_inc(compared, 1)
                        else:
                            dve.wait_ge(signed, g * DONE["A"][BANKS] + DONE["A"][b] + 1)
                            f = far[:, p].unsqueeze(1).broadcast_to([P, 4, P])
                            ins = dve.tensor_tensor(out=cmp, in0=signs[:, DONE["A"][b] % SIGNS], in1=f, op=ALU.is_gt)
                            ins.then_inc(cmp_done, 1)
                        if n == 24 and not (isinstance(i, int) and i == PAIRS - 1 and p == 1):
                            masks(i + p, 1 - p)
            pair_loop(dve, body)

        FIRST_HIGH = next(n for n in range(BANKS) if 4 * ORDER[n] >= P)

        @block.tensor
        def _(pe):
            def project(i, p, k):
                g = 2 * i + p
                if k == 0:
                    pe.wait_ge(x_in[p], 16 * (i + 1))
                    pe.matmul(scratch[:, 0:P], wuv[:, 0:P], xTg[:, p], start=True, stop=True)
                    pe.matmul(scratch[0:64, P:2 * P], wuv[:, P:HID], xTg[:, p], start=True, stop=True).then_inc(uv_ps, 1)
                if k == 1:
                    pe.wait_ge(uv_sb, 4 * g + 2)
                    pe.matmul(scratch[:, 0:HID], xTg[:, p], wuv[:, HID:2 * HID], start=True, stop=True).then_inc(uv_ps, 1)
                if k == 2:
                    pe.wait_ge(uv_sb, 4 * g + 3)
                    pe.matmul(scratch[:, 0:HID], xTg[:, p], wuv[:, 0:HID], start=True, stop=True).then_inc(uv_ps, 1)

            pe.wait_ge(w_in, 32)
            pe.wait_ge(set_, 5)
            pe.wait_ge(set_gp, 3)
            for k in range(3):
                project(0, 0, k)

            def reduce(g, p, n):
                b = ORDER[n]
                k = KINDS[b % 16]
                pe.wait_ge(compared if k == "D" else cmp_done, g * DONE[k][BANKS] + DONE[k][b] + 1)
                if n == 0:
                    pe.wait_ge(pool, g * POOL + 10)
                    after(pe, sums_done, g, 1, 0)
                if n == FIRST_HIGH and not (isinstance(g, int) and g == B - 1):
                    pe.wait_ge(uv_sb, 4 * (g + 2))
                for h in range(4):
                    ins = pe.matmul(red[:, 4 * b + h], cmps[:, n % CMPS, h], one_v[:, p, 4 * b + h], start=True, stop=True)
                ins.then_inc(reduced, 1)

            def body(i):
                for p in range(2):
                    g = 2 * i + p
                    pe.wait_ge(rows_in[p], ROWS_IN * (i + 1))
                    pe.wait_ge(masked, 2 * (g + 1))
                    for b in range(BANKS):
                        k = KINDS[(b - RING) % 16]
                        after(pe, compared if k == "D" else signed, g, DONE[k][BANKS],
                              DONE[k][b - RING] + 1 if b >= RING else DONE[k][b - RING + BANKS] + 1 - DONE[k][BANKS])
                        q, c = divmod(4 * b, SPAN)
                        mine = KINDS[b % 16] == "D"
                        ins = pe.matmul(bank[:, b % RING], t.pick[:, q], rows[:, p, c * P:(c + 4) * P], start=True, stop=not mine)
                        if mine:
                            ins = pe.matmul(bank[:, b % RING], t.eyeb[:], away[:, p].unsqueeze(1).broadcast_to([P, 4, P]),
                                            start=False, stop=True)
                        ins.then_inc(bcast, 1)
                        if b >= RED_LAG:
                            reduce(g, p, b - RED_LAG)
                        elif not (isinstance(g, int) and g == 0):
                            reduce(g - 1, 1 - p, b - RED_LAG + BANKS)
                        if b in PROJECT_AT and not (isinstance(i, int) and i == PAIRS - 1 and p == 1):
                            project(i + p, 1 - p, PROJECT_AT.index(b))
            pair_loop(pe, body)
            for n in range(BANKS - RED_LAG, BANKS):
                reduce(B - 1, 1, n)


def edge_out(nc, t, W2, b2):
    N = 4
    with ExitStack() as ctx:
        sb = lambda n, s, d: ctx.enter_context(nc.sbuf_tensor(n, s, d))
        pb = lambda n, s, d: ctx.enter_context(nc.psum_tensor(n, s, d))
        sem = lambda n: ctx.enter_context(nc.semaphore(n))
        w2 = sb("w2", [P, 2, C], F32)
        b2b = sb("b2b", [P, C], F32)
        stage = sb("stage", [P, 2, N, HID], F32)
        nil = sb("nilo", [P, N, HID], F32)
        set_gp, biased = sem("o_set_gp"), sem("o_biased")
        hT = sb("hT", [P, 2, N, P], F32)
        square = sb("square", [P, B, C], F32)
        stat, std = sb("stat", [P, 2, B], F32), sb("std", [P, B], F32)
        hTp = pb("hTp", [P, 2, 2, N, P], F32)
        y = pb("y", [P, 2, 512], F32)
        w_in, staged, turned, copied, made, work, ready, rooted = (
            sem("o_" + n) for n in ("w_in", "staged", "turned", "copied", "made", "work", "ready", "rooted"))
        block = ctx.enter_context(nc.Block())

        @block.sync
        def _(sp):
            sp.dma_start(w2[:, 0], W2[0:P]).then_inc(w_in, 16)
            sp.dma_start(w2[0:C, 1], W2[P:HID]).then_inc(w_in, 16)
            sp.dma_start(b2b[:], b2).then_inc(w_in, 16)

        def rounds(eng, body):
            for j in range(2):
                body(j, j)
            with eng.Fori(1, B // N // 2) as i:
                for p in range(2):
                    body(2 * i + p, p)

        @block.gpsimd
        def _(gp):
            gp.memset(nil[:], 0.0).then_inc(set_gp, 1)
            gp.wait_ge(set_gp, 1)

            def body(j, p):
                if not isinstance(j, int):
                    gp.wait_ge(turned, j - 1)
                gp.tensor_tensor(out=stage[:, p], in0=t.hm[:, bass.ds(j * N, N)], in1=nil[:], op=ALU.add).then_inc(staged, 1)
            rounds(gp, body)

        @block.tensor
        def _(pe):
            pe.wait_ge(w_in, 48)

            def body(j, p):
                pe.wait_ge(staged, j + 1)
                if not isinstance(j, int):
                    pe.wait_ge(copied, 2 * (j - 1))
                for g in range(N):
                    pe.transpose(hTp[:, p, 0, g], stage[:, p, g, 0:P], t.eye[:])
                    last = pe.transpose(hTp[0:C, p, 1, g], stage[:, p, g, P:HID], t.eye[:])
                last.then_inc(turned, 1)
                pe.wait_ge(copied, 2 * (j + 1))
                if not isinstance(j, int):
                    pe.wait_ge(work, 2 * (j - 1))
                for g in range(N):
                    pe.matmul(y[:, p, g * C:(g + 1) * C], hT[:, 0, g], w2[:, 0], start=True, stop=False)
                    last = pe.matmul(y[:, p, g * C:(g + 1) * C], hT[0:C, 1, g], w2[0:C, 1], start=False, stop=True)
                last.then_inc(made, 1)
            rounds(pe, body)

        @block.scalar
        def _(act):
            def body(j, p):
                act.wait_ge(turned, j + 1)
                if not (isinstance(j, int) and j == 0):
                    act.wait_ge(made, j)
                act.copy(hT[:, 0], hTp[:, p, 0]).then_inc(copied, 1)
                act.copy(hT[0:C, 1], hTp[0:C, p, 1]).then_inc(copied, 1)
            rounds(act, body)
            act.wait_ge(ready, 1)
            act.activation(std[:], stat[:, 1, :], ACT.Sqrt).then_inc(rooted, 1)

        @block.vector
        def _(dve):
            dve.wait_ge(w_in, 48)

            def body(j, p):
                link = chain(dve, work, 2 * j)
                here = bass.ds(j * N, N)
                if isinstance(j, int) and j == 0:
                    db = dve.tensor_tensor(out=square[:], in0=b2b[:].unsqueeze(1).broadcast_to([P, B, C]),
                                           in1=t.degree[:].unsqueeze(2).broadcast_to([P, B, C]), op=ALU.mult)
                    db.then_inc(biased, 1)
                    dve.wait_ge(biased, 1)
                link(dve.tensor_tensor(out=t.xs[:, here], in0=t.xs[:, here], in1=square[:, here], op=ALU.add))
                dve.wait_ge(made, j + 1)
                link(dve.tensor_tensor(out=t.xs[:, here], in0=t.xs[:, here],
                                       in1=y[:, p, 0:N * C].rearrange("p (g c) -> p g c", g=N), op=ALU.add))
            rounds(dve, body)
            link = chain(dve, work, 2 * (B // N))
            layer_norm(dve, link, t.xs, square, stat, std, ready, rooted, 1)


def rounds(eng, n, body):
    for j in range(2):
        body(j, j)
    with eng.Fori(1, n // 2) as i:
        for p in range(2):
            body(2 * i + p, p)


def at_least(eng, sem, v):
    if not isinstance(v, int) or v > 0:
        eng.wait_ge(sem, v)


def graph_conv(nc, t, W, gamma, beta, b):
    N = 4
    ROUNDS = B // N
    with ExitStack() as ctx:
        sb = lambda n, s, d: ctx.enter_context(nc.sbuf_tensor("c_" + n, s, d))
        pb = lambda n, s, d: ctx.enter_context(nc.psum_tensor("c_" + n, s, d))
        sem = lambda n: ctx.enter_context(nc.semaphore("c_" + n))
        w = sb("w", [P, 2, C], F32)
        gammab, betab, bb = (sb(n, [P, C], F32) for n in ("gamma", "beta", "bb"))
        hn, square = sb("hn", [P, B, C], F32), sb("square", [P, B, C], F32)
        stat, std = sb("stat", [P, 2, B], F32), sb("std", [P, B], F32)
        norm, nstd = sb("norm", [P, 2, C], F32), sb("nstd", [P, C], F32)
        root, iroot = sb("root", [P, B], F32), sb("iroot", [P, B], F32)
        hstage = sb("hstage", [P, 2, N, C], F32)
        astage = sb("astage", [P, 2, N, P], F32)
        nil = sb("nil", [P, N, P], F32)
        hT = sb("hT", [P, 2, N // 2, P], F32)
        xw, yw, z2 = sb("xw", [P, 2, N, C], F32), sb("yw", [P, 2, N, C], F32), sb("z2", [P, N, C], F32)
        sump = pb("sump", [P, 8, C], F32)
        hTp = pb("hTp", [P, 2, 512], F32)
        xp, zp = pb("xp", [P, 2, 512], F32), pb("zp", [P, 2, 512], F32)
        w_in, set_gp, work, summed, ready, rooted, staged, turned, copied, made_x, made_y, made_z, done, biased, added, set_w = (
            sem(n) for n in ("w_in", "set_gp", "work", "summed", "ready", "rooted", "staged", "turned", "copied",
                             "made_x", "made_y", "made_z", "done", "biased", "added", "set_w"))
        block = ctx.enter_context(nc.Block())

        @block.sync
        def _(sp):
            sp.wait_ge(set_w, 1)
            for h in range(2):
                sp.dma_start(w[C * h:C * h + C, h], W).then_inc(w_in, 16)
            for dst, src in ((gammab, gamma), (betab, beta), (bb, b)):
                sp.dma_start(dst[:], src).then_inc(w_in, 16)

        @block.gpsimd
        def _(gp):
            gp.memset(nil[:], 0.0).then_inc(set_gp, 1)
            gp.wait_ge(set_gp, 1)
            gp.wait_ge(work, 10)

            def body(j, p):
                at_least(gp, turned, j - 1)
                gp.tensor_tensor(out=hstage[:, p], in0=hn[:, bass.ds(j * N, N)], in1=nil[:, :, 0:C], op=ALU.add).then_inc(staged, 1)
                at_least(gp, made_z, j - 1)
                gp.tensor_tensor(out=astage[:, p], in0=t.adjT[:, bass.ds(j * N, N)], in1=nil[:], op=ALU.add).then_inc(staged, 1)
            rounds(gp, ROUNDS, body)

        @block.tensor
        def _(pe):
            for j in range(8):
                last = pe.matmul(sump[:], t.onesf[:], t.xs[:, 8 * j:8 * j + 8], start=(j == 0), stop=(j == 7))
            last.then_inc(summed, 1)
            pe.wait_ge(work, 4)
            for j in range(8):
                last = pe.matmul(sump[:], t.onesf[:], square[:, 8 * j:8 * j + 8], start=(j == 0), stop=(j == 7))
            last.then_inc(summed, 1)
            pe.wait_ge(w_in, 80)

            def neighbours_sum(j, p):
                pe.wait_ge(made_y, j + 1)
                at_least(pe, done, j - 1)
                for g in range(N):
                    last = pe.matmul(zp[:, p, g * C:(g + 1) * C], astage[:, p, g], yw[:, p, g], start=True, stop=True)
                last.then_inc(made_z, 1)

            def body(j, p):
                pe.wait_ge(staged, 2 * (j + 1))
                at_least(pe, copied, j - 1)
                for g in range(N // 2):
                    last = pe.transpose(hTp[:, p, g * P:(g + 1) * P], hstage[:, p, 2 * g:2 * g + 2].rearrange("p g c -> p (g c)"), t.eye[:])
                last.then_inc(turned, 1)
                pe.wait_ge(copied, j + 1)
                at_least(pe, made_y, j - 1)
                for g in range(N // 2):
                    last = pe.matmul(xp[:, p, g * P:(g + 1) * P], hT[:, p, g], w[:], start=True, stop=True)
                last.then_inc(made_x, 1)
                if not (isinstance(j, int) and j == 0):
                    neighbours_sum(j - 1, 1 - p)
            rounds(pe, ROUNDS, body)
            neighbours_sum(ROUNDS - 1, (ROUNDS - 1) % 2)

        @block.scalar
        def _(act):
            act.activation(root[:], t.rowsum[:], ACT.Sqrt).then_inc(rooted, 1)
            act.wait_ge(ready, 1)
            act.activation(nstd[:], norm[:, 1], ACT.Sqrt).then_inc(rooted, 1)

            def body(j, p):
                act.wait_ge(turned, j + 1)
                at_least(act, made_x, j - 1)
                act.copy(hT[:, p].rearrange("p g k -> p (g k)"), hTp[:, p, 0:N // 2 * P]).then_inc(copied, 1)
            rounds(act, ROUNDS, body)
            act.wait_ge(ready, 2)
            act.activation(std[:], stat[:, 1, :], ACT.Sqrt).then_inc(rooted, 1)

        @block.vector
        def _(dve):
            dve.memset(w[:], 0.0).then_inc(set_w, 1)
            link = chain(dve, work, 0)
            by_channel = lambda v: v.rearrange("p g c -> p c g")
            over = lambda v: v.unsqueeze(1).broadcast_to([P, B, C])
            dve.wait_ge(summed, 1)
            link(dve.tensor_reduce(norm[:, 0], by_channel(sump[:]), AX.X, ALU.add))
            link(dve.tensor_scalar(norm[:, 0], norm[:, 0], 1.0 / (B * P), None, ALU.mult))
            link(dve.tensor_tensor(out=hn[:], in0=t.xs[:], in1=over(norm[:, 0]), op=ALU.subtract))
            link(dve.tensor_tensor(out=square[:], in0=hn[:], in1=hn[:], op=ALU.mult))
            dve.wait_ge(summed, 2)
            link(dve.tensor_reduce(norm[:, 0], by_channel(sump[:]), AX.X, ALU.add))
            dve.tensor_scalar(norm[:, 1], norm[:, 0], 1.0 / (B * P), EPS, ALU.mult, ALU.add).then_inc(ready, 1)
            dve.wait_ge(rooted, 2)
            dve.wait_ge(w_in, 80)
            link(dve.reciprocal(norm[:, 0], nstd[:]))
            link(dve.tensor_tensor(out=norm[:, 0], in0=norm[:, 0], in1=gammab[:], op=ALU.mult))
            link(dve.tensor_tensor(out=hn[:], in0=hn[:], in1=over(norm[:, 0]), op=ALU.mult))
            link(dve.reciprocal(iroot[:], root[:]))
            assert link(dve.tensor_tensor(out=hn[:], in0=hn[:], in1=over(betab[:]), op=ALU.add)) == 10
            wide = lambda v: v.unsqueeze(2).broadcast_to([P, N, C])

            def scale_in(j, p):
                dve.wait_ge(made_x, j + 1)
                if not (isinstance(j, int) and j < 2):
                    dve.wait_ge(done, j - 1)
                x = dve.tensor_tensor(out=xw[:, p], in0=xp[:, p, 0:N * C].rearrange("p (g c) -> p g c", g=N),
                                      in1=bb[:].unsqueeze(1).broadcast_to([P, N, C]), op=ALU.add)
                x.then_inc(biased, 1)
                dve.wait_ge(biased, j + 1)
                at_least(dve, made_z, j - 1)
                dve.tensor_tensor(out=yw[:, p], in0=xw[:, p], in1=wide(iroot[:, bass.ds(j * N, N)]), op=ALU.mult).then_inc(made_y, 1)

            def add_up(j, p):
                link = chain(dve, added, 3 * j)
                here = bass.ds(j * N, N)
                dve.wait_ge(made_z, j + 1)
                link(dve.tensor_tensor(out=z2[:], in0=zp[:, p, 0:N * C].rearrange("p (g c) -> p g c", g=N),
                                       in1=wide(root[:, here]), op=ALU.mult))
                link(dve.tensor_tensor(out=z2[:], in0=xw[:, p], in1=z2[:], op=ALU.subtract))
                link(dve.scalar_tensor_tensor(out=z2[:], in0=z2[:], scalar=0.01, in1=z2[:], op0=ALU.mult, op1=ALU.max))
                dve.tensor_tensor(out=t.xs[:, here], in0=t.xs[:, here], in1=z2[:], op=ALU.add).then_inc(done, 1)
                dve.wait_ge(done, j + 1)

            def body(j, p):
                scale_in(j, p)
                if not (isinstance(j, int) and j == 0):
                    add_up(j - 1, 1 - p)
            rounds(dve, ROUNDS, body)
            add_up(ROUNDS - 1, (ROUNDS - 1) % 2)
            link = chain(dve, work, 10)
            layer_norm(dve, link, t.xs, square, stat, std, ready, rooted, 3)


def sort_columns(nc, t):
    TURNS = PAIRS // 2
    LOW = -3.0e38
    with ExitStack() as ctx:
        sb = lambda n, s, d: ctx.enter_context(nc.sbuf_tensor("s_" + n, s, d))
        pb = lambda n, s, d: ctx.enter_context(nc.psum_tensor("s_" + n, s, d))
        sem = lambda n: ctx.enter_context(nc.semaphore("s_" + n))
        stage = sb("stage", [P, 2, 2 * C], F32)
        rest = sb("rest", [P, 2, P], F32)
        top = sb("top", [P, 2, P], F32)
        tick = sb("tick", [P, 2], F32)
        S = sb("S", [P, PAIRS, P + 1], F32)
        gap = sb("gap", [P, PAIRS, P], F32)
        resid = sb("resid", [P, PAIRS, P], F32)
        gstage = sb("gstage", [P, 2, 4, P], F32)
        colp = pb("colp", [P, 2, 512], F32)
        gapp = pb("gapp", [P, 2, 4, P], F32)
        gapT = S[:].rearrange("p a q -> p (a q)")[:, 0:PAIRS * P].rearrange("p (a q) -> p a q", q=P)
        staged, turned, work, gstaged, gturned, gkept, split = (
            sem(n) for n in ("staged", "turned", "work", "gstaged", "gturned", "gkept", "split"))
        PER = 2 + 16 * 2 + 15 * 2 + 31 + 2
        block = ctx.enter_context(nc.Block())

        @block.scalar
        def _(act):
            def body(i, first):
                for p in range(2):
                    if not first:
                        act.wait_ge(turned, 2 * i + p - 1)
                    pair = bass.ds(4 * i + 2 * p, 2)
                    act.copy(stage[:, p].rearrange("k (g c) -> k g c", g=2), t.xs[:, pair]).then_inc(staged, 1)
            body(0, True)
            with act.Fori(1, TURNS) as i:
                body(i, False)
            act.wait_ge(split, 7)

            def turn(j, p):
                act.wait_ge(gturned, j + 1)
                act.mul(gapT[:, bass.ds(4 * j, 4)], gapp[:, p], 0.25).then_inc(gkept, 1)
            rounds(act, PAIRS // 4, turn)

        @block.gpsimd
        def _(gp):
            gp.wait_ge(split, 2)

            def turn(j, p):
                at_least(gp, gturned, j - 1)
                gp.tensor_copy(gstage[:, p], gap[:, bass.ds(4 * j, 4)]).then_inc(gstaged, 1)
            for j in range(PAIRS // 4):
                turn(j, j % 2)

        @block.tensor
        def _(pe):
            def body(i, first):
                for p in range(2):
                    pe.wait_ge(staged, 2 * i + p + 1)
                    if not first:
                        pe.wait_ge(work, i * PER - PER + 3)
                    pe.transpose(colp[:, p, 0:P], stage[:, p], t.eye[:]).then_inc(turned, 1)
            body(0, True)
            with pe.Fori(1, TURNS) as i:
                body(i, False)

            def turn(j, p):
                pe.wait_ge(gstaged, j + 1)
                at_least(pe, gkept, j - 1)
                for n in range(4):
                    last = pe.transpose(gapp[:, p, n], gstage[:, p, n], t.eye[:])
                last.then_inc(gturned, 1)
            rounds(pe, PAIRS // 4, turn)

        @block.vector
        def _(dve):
            dve.memset(S[:, :, 0], TOP).then_inc(work, 1)
            with dve.Fori(0, TURNS) as i:
                n = 0

                def count(ins):
                    nonlocal n
                    ins.then_inc(work, 1)
                    n += 1

                def settle():
                    dve.wait_ge(work, i * PER + n + 1)
                    count(dve.memset(tick[:], 0.0))

                dve.wait_ge(work, i * PER + 1)
                dve.wait_ge(turned, 2 * i + 2)
                for p in range(2):
                    count(dve.tensor_copy(rest[:, p], colp[:, p, 0:P]))
                for r in range(16):
                    settle()
                    for p in range(2):
                        count(dve.max(top[:, p, 8 * r:8 * r + 8], rest[:, p]))
                    if r < 15:
                        settle()
                        for p in range(2):
                            count(dve.match_replace(rest[:, p], top[:, p, 8 * r:8 * r + 8], rest[:, p], LOW))
                dve.wait_ge(work, i * PER + n + 1)
                for p in range(2):
                    count(dve.tensor_copy(S[:, bass.ds(2 * i + p, 1), 1:P + 1].rearrange("p o q -> p (o q)"), top[:, p]))
                assert n == PER, n
            dve.wait_ge(work, TURNS * PER + 1)
            link = chain(dve, split, 0)
            link(dve.tensor_tensor(out=gap[:, :, 1:P], in0=S[:, :, 2:P + 1], in1=S[:, :, 1:P], op=ALU.subtract))
            link(dve.tensor_copy(gap[:, :, 0], S[:, :, 1]))
            s = S[:, :, 0:P]
            link(dve.tensor_copy(t.Sparts[:, 0], s))
            link(dve.tensor_tensor(out=resid[:], in0=s, in1=t.Sparts[:, 0], op=ALU.subtract))
            link(dve.tensor_copy(t.Sparts[:, 1], resid[:]))
            link(dve.tensor_tensor(out=resid[:], in0=resid[:], in1=t.Sparts[:, 1], op=ALU.subtract))
            assert link(dve.tensor_copy(t.Sparts[:, 2], resid[:])) == 7
            dve.wait_ge(gkept, PAIRS // 4)
            link(dve.tensor_copy(t.gaps[:, :, :, 0], gapT))
            link(dve.tensor_tensor(out=resid[:], in0=gapT, in1=t.gaps[:, :, :, 0], op=ALU.subtract))
            link(dve.tensor_copy(t.gaps[:, :, :, 1], resid[:]))
            link(dve.tensor_tensor(out=resid[:], in0=resid[:], in1=t.gaps[:, :, :, 1], op=ALU.subtract))
            link(dve.tensor_copy(t.gaps[:, :, :, 2], resid[:]))


SETS = C // 4
TILES = C // 2
TYPE = ["AANAANAANAANAANA"[n % 16] for n in range(TILES)]
CLIP_LAG = 6
ABOVE, COPIES, CLIPS = 4, 4, 8


def quantiles(nc, t):
    with ExitStack() as ctx:
        sb = lambda n, s, d: ctx.enter_context(nc.sbuf_tensor("q_" + n, s, d))
        pb = lambda n, s, d: ctx.enter_context(nc.psum_tensor("q_" + n, s, d))
        sem = lambda n: ctx.enter_context(nc.semaphore("q_" + n))
        SPAN = C // 4
        rows = sb("rows", [P, 2, SPAN * P], BF16)
        left = sb("left", [P, 3, P], BF16)
        base = sb("base", [P, 2, 3, P], BF16)
        pos1 = sb("pos1", [P, 2, 3, P], F16)
        nv = sb("nv", [P, 2, P], BF16)
        xg = sb("xg", [P, 2, C], F32)
        gap1, gap2 = sb("gap1", [P, 2, C, 3], BF16), sb("gap2", [P, 2, C, 3], BF16)
        nil = sb("nil", [P, C, 3], BF16)
        above = sb("above", [P, ABOVE, 4, P], BF16)
        copies = sb("copies", [P, COPIES, 2, 3, P], BF16)
        shifted = sb("shifted", [P, 2, 2, 3, P], BF16)
        clips = sb("clips", [P, CLIPS, 2, 3, P], BF16)
        srow = pb("srow", [P, 2, 4, P], F32)
        cnt = pb("cnt", [P, 2, 2, 512], F32)
        aggp = pb("aggp", [P, 2, 512], F32)
        set_, set_gp, prep, prep_gp, summed, based, bcast, compared, counted, taken, moved, clipped, reduced, kept = (
            sem(n) for n in ("set", "set_gp", "prep", "prep_gp", "summed", "based", "bcast", "compared", "counted", "taken",
                             "moved", "clipped", "reduced", "kept"))
        rows_in = [sem(f"rows_in{p}") for p in range(2)]
        MOVES = TYPE.count("N")
        move = [TYPE[:n].count("N") for n in range(TILES)]
        block = ctx.enter_context(nc.Block())

        def pair_loop(eng, body):
            body(0)
            with eng.Fori(1, PAIRS - 1) as i:
                body(i)
            body(PAIRS - 1)

        starts = lambda g: isinstance(g, int) and g == 0
        ends = lambda i, p: isinstance(i, int) and i == PAIRS - 1 and p == 1

        @block.sync
        def _(sp):
            def flatten(i, p):
                g = 2 * i + p
                at_least(sp, bcast, (g - 1) * SETS)
                for s in range(3):
                    for q in range(4):
                        at = 64 * p + SPAN * q
                        sp.dma_start(rows[32 * q + s:32 * q + s + 1, p, :].rearrange("o (c k) -> o c k", c=SPAN),
                                     t.Sparts[at:at + SPAN, s, bass.ds(i, 1), :].rearrange("c o k -> c (o k)")).then_inc(rows_in[p], 16)
            sp.wait_ge(set_, 4)
            flatten(0, 0)

            def body(i):
                for p in range(2):
                    if not ends(i, p):
                        flatten(i + p, 1 - p)
            pair_loop(sp, body)

        @block.gpsimd
        def _(gp):
            gp.memset(nil[:], 0.0).then_inc(set_gp, 1)
            gp.wait_ge(set_gp, 1)

            def prepare(i, p):
                g = 2 * i + p
                at_least(gp, compared, (g - 1) * SETS)
                at_least(gp, reduced, (g - 1) * TILES)
                gp.tensor_tensor(out=xg[:, p], in0=t.xs[:, bass.ds(g, 1), :].rearrange("p o c -> p (o c)"), in1=nil[:, :, 0],
                                 op=ALU.add).then_inc(prep_gp, 1)
                gaps = t.gaps[:, bass.ds(i, 1), C * p:C * p + C, :].rearrange("p o c s -> p (o c) s")
                gp.tensor_tensor(out=gap1[:, p], in0=gaps, in1=nil[:], op=ALU.add).then_inc(prep_gp, 1)
                gp.tensor_tensor(out=gap2[:, p], in0=gaps, in1=gaps, op=ALU.add).then_inc(prep_gp, 1)
            prepare(0, 0)

            def body(i):
                for p in range(2):
                    if not ends(i, p):
                        prepare(i + p, 1 - p)
            pair_loop(gp, body)

        @block.scalar
        def _(act):
            def body(i):
                for p in range(2):
                    g = 2 * i + p
                    for n in range(TILES):
                        act.wait_ge(counted, g * TILES + n + 1)
                        b = n - COPIES
                        if TYPE[b] == "A":
                            at_least(act, clipped, g * TILES + b + 1)
                        else:
                            at_least(act, moved, (g if b >= 0 else g - 1) * MOVES + move[b] + 1)
                        if TYPE[n] == "A":
                            act.copy(copies[:, n % COPIES].rearrange("p c s i -> p c (s i)"), cnt[:, n % 2, :, 0:3 * P]).then_inc(taken, 1)
                        else:
                            act.copy(copies[:, n % COPIES, :, 0], cnt[:, n % 2, :, 0:P]).then_inc(taken, 1)
            pair_loop(act, body)

        @block.vector
        def _(dve):
            for n, tau in enumerate(TAUS):
                dve.tensor_scalar(left[:, n], t.eye[:], 1.0 - tau, None, ALU.mult).then_inc(set_, 1)
            dve.memset(rows[:], 0.0).then_inc(set_, 1)
            dve.wait_ge(set_, 3)

            def prepare(i, p):
                g = 2 * i + p
                at_least(dve, counted, (g - 1) * TILES)
                v = t.negV[:, bass.ds(g, 1), :].rearrange("p o k -> p (o k)")
                dve.tensor_copy(nv[:, p], v).then_inc(prep, 1)
                for n, tau in enumerate(TAUS):
                    dve.scalar_tensor_tensor(out=base[:, p, n], in0=v, scalar=-tau, in1=left[:, n],
                                             op0=ALU.mult, op1=ALU.add).then_inc(prep, 1)

            def positions(i, p):
                g = 2 * i + p
                dve.wait_ge(summed, g + 1)
                at_least(dve, moved, (g - 1) * MOVES)
                for n, tau in enumerate(TAUS):
                    dve.tensor_scalar(pos1[:, p, n], aggp[:, p, 256:256 + P], -tau, 1.0 - tau, ALU.mult, ALU.add).then_inc(based, 1)

            def compare(g, p, s):
                if s == 0:
                    dve.wait_ge(prep_gp, 3 * g + 1)
                dve.wait_ge(bcast, g * SETS + s + 1)
                at_least(dve, counted, g * TILES + 2 * (s - ABOVE + 1))
                x = xg[:, p, 4 * s:4 * s + 4].unsqueeze(2).broadcast_to([P, 4, P])
                dve.tensor_tensor(out=above[:, s % ABOVE], in0=srow[:, s % 2], in1=x, op=ALU.is_le).then_inc(compared, 1)

            def keep(g, p):
                dve.wait_ge(reduced, (g + 1) * TILES)
                dve.tensor_reduce(t.agg[:, bass.ds(g, 1), :].rearrange("p o c -> p (o c)"),
                                  aggp[:, p, 0:3 * C].rearrange("p (c s) -> p c s", s=3), AX.X, ALU.add).then_inc(kept, 1)

            def shift(g, p, n):
                if n == move.index(0):
                    dve.wait_ge(based, 3 * (g + 1))
                dve.wait_ge(taken, g * TILES + n + 1)
                at_least(dve, clipped, g * TILES + n - 1)
                dve.tensor_tensor(out=shifted[:, n % 2], in0=copies[:, n % COPIES, :, 0].unsqueeze(2).broadcast_to([P, 2, 3, P]),
                                  in1=pos1[:, p].unsqueeze(1).broadcast_to([P, 2, 3, P]), op=ALU.add).then_inc(moved, 1)

            def clip(g, n):
                at_least(dve, reduced, g * TILES + n - CLIPS + 1)
                if TYPE[n] == "A":
                    dve.wait_ge(taken, g * TILES + n + 1)
                    src = copies[:, n % COPIES]
                else:
                    dve.wait_ge(moved, g * MOVES + move[n] + 1)
                    src = shifted[:, n % 2]
                dve.tensor_scalar(clips[:, n % CLIPS], src, 0.0, 1.0, ALU.max, ALU.min).then_inc(clipped, 1)

            prepare(0, 0)
            positions(0, 0)
            compare(0, 0, 0)
            compare(0, 0, 1)

            def body(i):
                for p in range(2):
                    g = 2 * i + p
                    for n in range(TILES):
                        if n % 2 == 0:
                            s = n // 2 + 2
                            if s < SETS:
                                compare(g, p, s)
                            elif not ends(i, p):
                                compare(g + 1, 1 - p, s - SETS)
                        if TYPE[n] == "N":
                            shift(g, p, n)
                        if n > 0:
                            clip(g, n - 1)
                        elif not starts(g):
                            clip(g - 1, TILES - 1)
                        if n == 10 and not starts(g):
                            keep(g - 1, 1 - p)
                        if n == 14 and not ends(i, p):
                            prepare(i + p, 1 - p)
                        if n == 22 and not ends(i, p):
                            positions(i + p, 1 - p)
            pair_loop(dve, body)
            clip(B - 1, TILES - 1)
            keep(B - 1, 1)

        @block.tensor
        def _(pe):
            def broadcast(i, p, s):
                g = 2 * i + p
                if s == 0:
                    pe.wait_ge(rows_in[p], 192 * (i + 1))
                at_least(pe, compared, g * SETS + s - 1)
                q, c = divmod(4 * s, SPAN)
                pe.matmul(srow[:, s % 2], t.pick[:, q], rows[:, p, c * P:(c + 4) * P], start=True, stop=True).then_inc(bcast, 1)

            def neighbours_of(i, p):
                g = 2 * i + p
                pe.wait_ge(prep, 4 * (g + 1))
                at_least(pe, kept, g - 1)
                pe.matmul(aggp[:, p, 256:256 + P], t.ones[:], nv[:, p], start=True, stop=True).then_inc(summed, 1)

            def count(g, p, n):
                s = n // 2
                if n % 2 == 0:
                    pe.wait_ge(compared, g * SETS + s + 1)
                at_least(pe, taken, g * TILES + n - 1)
                if TYPE[n] == "A":
                    for h in range(2):
                        pe.matmul(cnt[:, n % 2, h, 0:3 * P], t.ones[:], base[:, p], start=True, stop=False)
                for h in range(2):
                    m = above[:, s % ABOVE, 2 * (n % 2) + h]
                    if TYPE[n] == "A":
                        last = pe.matmul(cnt[:, n % 2, h, 0:3 * P], m, nv[:, p].unsqueeze(1).broadcast_to([P, 3, P]), start=False, stop=True)
                    else:
                        last = pe.matmul(cnt[:, n % 2, h, 0:P], m, nv[:, p], start=True, stop=True)
                last.then_inc(counted, 1)

            def reduce(g, p, n):
                if n == 0:
                    pe.wait_ge(prep_gp, 3 * (g + 1))
                    pe.wait_ge(based, 3 * (g + 1))
                pe.wait_ge(clipped, g * TILES + n + 1)
                for h in range(2):
                    c = 2 * n + h
                    for k in range(3):
                        last = pe.matmul(aggp[:, p, 3 * c:3 * c + 3], clips[:, n % CLIPS, h, k],
                                         (gap2 if k == 1 else gap1)[:, p, c], start=(k == 0), stop=(k == 2))
                last.then_inc(reduced, 1)

            pe.wait_ge(set_, 4)
            neighbours_of(0, 0)
            for s in range(3):
                broadcast(0, 0, s)

            def body(i):
                for p in range(2):
                    g = 2 * i + p
                    for n in range(TILES):
                        if n % 2 == 0:
                            s = n // 2 + 3
                            if s < SETS:
                                broadcast(i, p, s)
                            elif not ends(i, p):
                                broadcast(i + p, 1 - p, s - SETS)
                        count(g, p, n)
                        if n >= CLIP_LAG:
                            reduce(g, p, n - CLIP_LAG)
                        elif not starts(g):
                            reduce(g - 1, 1 - p, n - CLIP_LAG + TILES)
                        if n == 18 and not ends(i, p):
                            neighbours_of(i + p, 1 - p)
            pair_loop(pe, body)
            for n in range(TILES - CLIP_LAG, TILES):
                reduce(B - 1, 1, n)


def quantile_out(nc, t, W1, b1, W2, b2):
    N = 4
    ROUNDS = B // N
    H = P
    with ExitStack() as ctx:
        sb = lambda n, s, d: ctx.enter_context(nc.sbuf_tensor("m_" + n, s, d))
        pb = lambda n, s, d: ctx.enter_context(nc.psum_tensor("m_" + n, s, d))
        sem = lambda n: ctx.enter_context(nc.semaphore("m_" + n))
        w1, b1c, w2, b2b = sb("w1", [P, 2, H], F32), sb("b1c", [H, 1], F32), sb("w2", [H, C], F32), sb("b2b", [P, C], F32)
        square = sb("square", [P, B, C], F32)
        stat, std = sb("stat", [P, 2, B], F32), sb("std", [P, B], F32)
        stage = sb("stage", [P, 2, N, C], F32)
        oT, h = sb("oT", [P, 2, N // 2, P], F32), sb("h", [H, 2, 2, N // 2, P], F32)
        y2 = sb("y2", [P, N, C], F32)
        oTp, hp, yp = pb("oTp", [P, 2, 512], F32), pb("hp", [H, 2, 2, N // 2, P], F32), pb("yp", [P, 2, 512], F32)
        w_in, staged, turned, copied, hidden, rectified, made, added, done, work, ready, rooted, set_w = (
            sem(n) for n in ("w_in", "staged", "turned", "copied", "hidden", "rectified", "made", "added", "done", "work",
                             "ready", "rooted", "set_w"))
        block = ctx.enter_context(nc.Block())

        @block.sync
        def _(sp):
            sp.wait_ge(set_w, 1)
            for q in range(2):
                sp.dma_start(w1[C * q:C * q + C, q], W1).then_inc(w_in, 16)
            for dst, src in ((b1c, b1), (w2, W2), (b2b, b2)):
                sp.dma_start(dst[:], src).then_inc(w_in, 16)

        @block.gpsimd
        def _(gp):
            def body(j, p):
                here = bass.ds(j * N, N)
                at_least(gp, turned, j - 1)
                gp.tensor_tensor(out=stage[:, p], in0=t.xs[:, here], in1=t.agg[:, here], op=ALU.add).then_inc(staged, 1)
            rounds(gp, ROUNDS, body)

        @block.tensor
        def _(pe):
            pe.wait_ge(w_in, 80)

            def second(j, p):
                pe.wait_ge(rectified, j + 1)
                at_least(pe, added, j - 1)
                for g in range(N):
                    last = pe.matmul(yp[:, p, g * C:(g + 1) * C], h[:, p, g % 2, g // 2], w2[:], start=True, stop=True)
                last.then_inc(made, 1)

            def body(j, p):
                pe.wait_ge(staged, j + 1)
                at_least(pe, copied, j - 1)
                for g in range(N // 2):
                    last = pe.transpose(oTp[:, p, g * P:(g + 1) * P], stage[:, p, 2 * g:2 * g + 2].rearrange("p g c -> p (g c)"), t.eye[:])
                last.then_inc(turned, 1)
                pe.wait_ge(copied, j + 1)
                at_least(pe, rectified, j - 1)
                for q in range(2):
                    last = pe.matmul(hp[:, p, q], w1[:, q], oT[:, p], start=True, stop=True)
                last.then_inc(hidden, 1)
                if not (isinstance(j, int) and j == 0):
                    second(j - 1, 1 - p)
            rounds(pe, ROUNDS, body)
            second(ROUNDS - 1, 1)

        @block.scalar
        def _(act):
            act.wait_ge(w_in, 80)

            def body(j, p):
                act.wait_ge(turned, j + 1)
                at_least(act, hidden, j - 1)
                act.copy(oT[:, p].rearrange("p g k -> p (g k)"), oTp[:, p, 0:N // 2 * P]).then_inc(copied, 1)
                act.wait_ge(hidden, j + 1)
                at_least(act, made, j - 1)
                act.activation(h[:, p], hp[:, p], ACT.Relu, bias=b1c[:, 0:1]).then_inc(rectified, 1)
            rounds(act, ROUNDS, body)
            act.wait_ge(ready, 1)
            act.activation(std[:], stat[:, 1, :], ACT.Sqrt).then_inc(rooted, 1)

        @block.vector
        def _(dve):
            dve.memset(w1[:], 0.0).then_inc(set_w, 1)
            dve.wait_ge(w_in, 80)

            def body(j, p):
                here = bass.ds(j * N, N)
                dve.wait_ge(made, j + 1)
                dve.tensor_tensor(out=y2[:], in0=yp[:, p, 0:N * C].rearrange("p (g c) -> p g c", g=N),
                                  in1=b2b[:].unsqueeze(1).broadcast_to([P, N, C]), op=ALU.add).then_inc(added, 1)
                dve.wait_ge(added, j + 1)
                link = chain(dve, done, 2 * j)
                link(dve.tensor_tensor(out=y2[:], in0=y2[:], in1=t.maskf[:, here].unsqueeze(2).broadcast_to([P, N, C]), op=ALU.mult))
                at_least(dve, staged, j + 1)
                link(dve.tensor_tensor(out=t.xs[:, here], in0=t.xs[:, here], in1=y2[:], op=ALU.add))
            rounds(dve, ROUNDS, body)
            layer_norm(dve, chain(dve, work, 0), t.xs, square, stat, std, ready, rooted, 1)


def gru(nc, t, W1, b1, W2, b2, Wih, bih, Whh, bhh):
    N = 4
    ROUNDS = B // N
    with ExitStack() as ctx:
        sb = lambda n, s, d: ctx.enter_context(nc.sbuf_tensor("g_" + n, s, d))
        pb = lambda n, s, d: ctx.enter_context(nc.psum_tensor("g_" + n, s, d))
        sem = lambda n: ctx.enter_context(nc.semaphore("g_" + n))
        w1, b1c, w2, b2b = sb("w1", [P, 2, C], F32), sb("b1c", [P, 1], F32), sb("w2", [P, 2, C], F32), sb("b2b", [P, C], F32)
        wi, wh = sb("wi", [P, 2, 4, C], F32), sb("wh", [P, 2, 4, C], F32)
        bi, bh, bias = sb("bi", [P, 3, C], F32), sb("bh", [P, 3, C], F32), sb("bias", [P, 4, C], F32)
        square = sb("square", [P, B, C], F32)
        stat, std = sb("stat", [P, 2, B], F32), sb("std", [P, B], F32)
        stage = sb("stage", [P, 2, N, C], F32)
        nil = sb("nil", [P, N, C], F32)
        xT, mT, msgT = sb("xT", [P, 2, N // 2, P], F32), sb("mT", [P, N // 2, P], F32), sb("msgT", [P, N // 2, P], F32)
        m = sb("m", [P, N, C], F32)
        gates, th = sb("gates", [P, 2, N, 4, C], F32), sb("th", [P, 2, N, 2, C], F32)
        new = sb("new", [P, 2, N, C], F32)
        tanh_new = sb("tanh_new", [P, 2, N, C], F32)
        xTp, m1p, m2p, msgp = pb("xTp", [P, 512], F32), pb("m1p", [P, 512], F32), pb("m2p", [P, 512], F32), pb("msgp", [P, N // 2, 2, P], F32)
        gp_ = pb("gatesp", [P, 2, N, 4 * C], F32)
        (w_in, set_, set_gp, staged, turned, copied, made1, act1, made2, biased, act2, made3, act3, made4, gated, work,
         thalf, mixed, tnew, done, ready, rooted, lnwork, set_w) = (
            sem(n) for n in ("w_in", "set", "set_gp", "staged", "turned", "copied", "made1", "act1", "made2", "biased", "act2",
                             "made3", "act3", "made4", "gated", "work", "thalf", "mixed", "tnew", "done", "ready", "rooted", "lnwork", "set_w"))
        block = ctx.enter_context(nc.Block())

        def ahead(eng, front, body):
            front(0, 0)
            for j in range(2):
                body(j, j, True)
            with eng.Fori(1, ROUNDS // 2 - 1) as i:
                for p in range(2):
                    body(2 * i + p, p, True)
            body(ROUNDS - 2, 0, True)
            body(ROUNDS - 1, 1, False)

        @block.sync
        def _(sp):
            sp.wait_ge(set_w, 4)
            for q in range(2):
                at = slice(C * q, C * q + C)
                for dst, src in ((w1[at, q], W1), (b1c[at], b1), (w2[at, q], W2), (wi[at, q, 0:3], Wih),
                                 (wh[at, q, 0:2], Whh[:, 0:2]), (wh[at, q, 3], Whh[:, 2])):
                    sp.dma_start(dst, src).then_inc(w_in, 16)
            for dst, src in ((b2b, b2), (bi, bih), (bh, bhh)):
                sp.dma_start(dst[:], src).then_inc(w_in, 16)

        @block.gpsimd
        def _(gp):
            gp.memset(nil[:], 0.0).then_inc(set_gp, 1)
            gp.wait_ge(set_gp, 1)

            def body(j, p):
                at_least(gp, turned, j - 1)
                gp.tensor_tensor(out=stage[:, p], in0=t.xs[:, bass.ds(j * N, N)], in1=nil[:], op=ALU.add).then_inc(staged, 1)
            rounds(gp, ROUNDS, body)

        @block.tensor
        def _(pe):
            pe.wait_ge(w_in, 240)
            
            def gates_of(j, p):
                pe.wait_ge(act3, 2 * (j + 1))
                at_least(pe, gated, j - 1)
                for g in range(N // 2):
                    pe.matmul(gp_[:, p, 2 * g:2 * g + 2], msgT[:, g], wi[:].rearrange("p q a c -> p (q a c)"), start=True, stop=False)
                    last = pe.matmul(gp_[:, p, 2 * g:2 * g + 2], xT[:, p, g], wh[:].rearrange("p q a c -> p (q a c)"), start=False, stop=True)
                last.then_inc(made4, 1)

            def body(j, p):
                pe.wait_ge(staged, j + 1)
                at_least(pe, copied, j)
                for g in range(N // 2):
                    last = pe.transpose(xTp[:, g * P:(g + 1) * P], stage[:, p, 2 * g:2 * g + 2].rearrange("p g c -> p (g c)"), t.eye[:])
                last.then_inc(turned, 1)
                pe.wait_ge(copied, j + 1)
                at_least(pe, act1, j)
                pe.matmul(m1p[:, 0:N // 2 * P], w1[:], xT[:, p], start=True, stop=True).then_inc(made1, 1)
                pe.wait_ge(act1, j + 1)
                at_least(pe, biased, j)
                for g in range(N // 2):
                    last = pe.matmul(m2p[:, g * P:(g + 1) * P], mT[:, g], w2[:], start=True, stop=True)
                last.then_inc(made2, 1)
                pe.wait_ge(act2, j + 1)
                at_least(pe, act3, 2 * j)
                for g in range(N // 2):
                    last = pe.matmul(msgp[:, g], m[:, 2 * g:2 * g + 2].rearrange("p g c -> p (g c)"),
                                     t.adjT[:, bass.ds(j * N + 2 * g, 2), :], start=True, stop=True)
                last.then_inc(made3, 1)
                gates_of(j, p)
            rounds(pe, ROUNDS, body)

        @block.scalar
        def _(act):
            act.wait_ge(w_in, 240)

            def front(j, p):
                act.wait_ge(turned, j + 1)
                at_least(act, made4, j - 1)
                act.activation(xT[:, p].rearrange("p g k -> p (g k)"), xTp[:, 0:N // 2 * P], ACT.Copy).then_inc(copied, 1)
                act.wait_ge(made1, j + 1)
                at_least(act, made2, j)
                act.activation(mT[:].rearrange("p g k -> p (g k)"), m1p[:, 0:N // 2 * P], ACT.Relu, bias=b1c[:, 0:1]).then_inc(act1, 1)

            def body(j, p, more):
                act.wait_ge(made3, j + 1)
                at_least(act, made4, j)
                for q in range(2):
                    act.activation(msgT[C * q:C * q + C], msgp[C * q:C * q + C, :, q], ACT.Relu).then_inc(act3, 1)
                act.wait_ge(gated, j + 1)
                at_least(act, done, 6 * (j - 1))
                act.activation(th[:, p], gates[:, p, :, 0:2], ACT.Tanh, scale=0.5).then_inc(thalf, 1)
                if more:
                    front(j + 1, 1 - p)
                act.wait_ge(mixed, j + 1)
                act.activation(tanh_new[:, p], new[:, p], ACT.Tanh).then_inc(tnew, 1)
            ahead(act, front, body)
            act.wait_ge(ready, 1)
            act.activation(std[:], stat[:, 1, :], ACT.Sqrt).then_inc(rooted, 1)

        @block.vector
        def _(dve):
            for w in (w1, w2, wi, wh):
                dve.memset(w[:], 0.0).then_inc(set_w, 1)
            dve.wait_ge(w_in, 240)
            dve.tensor_tensor(out=bias[:, 0:2], in0=bi[:, 0:2], in1=bh[:, 0:2], op=ALU.add).then_inc(set_, 1)
            dve.tensor_copy(bias[:, 2], bi[:, 2]).then_inc(set_, 1)
            dve.tensor_copy(bias[:, 3], bh[:, 2]).then_inc(set_, 1)
            dve.wait_ge(set_, 3)

            def front(j, p):
                dve.wait_ge(made2, j + 1)
                at_least(dve, made3, j)
                dve.tensor_tensor(out=m[:], in0=m2p[:, 0:N * C].rearrange("p (g c) -> p g c", g=N),
                                  in1=b2b[:].unsqueeze(1).broadcast_to([P, N, C]), op=ALU.add).then_inc(biased, 1)
                dve.wait_ge(biased, j + 1)
                dve.tensor_scalar(m[:], m[:], 0.0, None, ALU.max).then_inc(act2, 1)

            def body(j, p, more):
                here = bass.ds(j * N, N)
                dve.wait_ge(made4, j + 1)
                dve.tensor_tensor(out=gates[:, p].rearrange("p g a c -> p g (a c)"), in0=gp_[:, p],
                                  in1=bias[:].rearrange("p a c -> p (a c)").unsqueeze(1).broadcast_to([P, N, 4 * C]),
                                  op=ALU.add).then_inc(gated, 1)
                link = chain(dve, done, 6 * j)
                dve.wait_ge(thalf, j + 1)
                sig, hn = th[:, p], gates[:, p, :, 3]
                link(dve.tensor_scalar(sig, sig, 0.5, 0.5, ALU.mult, ALU.add))
                link(dve.tensor_tensor(out=new[:, p], in0=sig[:, :, 0], in1=hn, op=ALU.mult))
                dve.tensor_tensor(out=new[:, p], in0=new[:, p], in1=gates[:, p, :, 2], op=ALU.add).then_inc(mixed, 1)
                if more:
                    front(j + 1, 1 - p)
                dve.wait_ge(tnew, j + 1)
                h, n = t.xs[:, here], tanh_new[:, p]
                link(dve.tensor_tensor(out=new[:, p], in0=h, in1=n, op=ALU.subtract))
                link(dve.tensor_tensor(out=new[:, p], in0=new[:, p], in1=sig[:, :, 1], op=ALU.mult))
                link(dve.tensor_tensor(out=new[:, p], in0=new[:, p], in1=n, op=ALU.add))
                dve.wait_ge(staged, j + 1)
                link(dve.tensor_tensor(out=t.xs[:, here], in0=h, in1=new[:, p], op=ALU.add))
            ahead(dve, front, body)
            layer_norm(dve, chain(dve, lnwork, 0), t.xs, square, stat, std, ready, rooted, 1)


def build(nc, d, out, stop=9):
    with ExitStack() as ctx:
        sb = lambda n, s, dt: ctx.enter_context(nc.sbuf_tensor(n, s, dt))

        class t:
            xs = sb("xs", [P, B, C], F32)
            adjT = sb("adjT", [P, B, P], F32)
            negV = sb("negV", [P, B, P], BF16)
            rowsum, degree, maskf = (sb(n, [P, B], F32) for n in ("rowsum", "degree", "maskf"))
            eye, onesf = sb("eye", [P, P], F32), sb("onesf", [P, P], F32)
            eyeb, ones = sb("eyeb", [P, P], BF16), sb("ones", [P, P], BF16)
            pick = sb("pick", [P, 4, P], BF16)

        neighbours(nc, t, d["adj"], d["adjT"], d["mask"], d["x"], d["ident"])
        with nc.sbuf_tensor("hm", [P, B, HID], F32) as hm:
            t.hm = hm
            edge_mlp(nc, t, d["xT"], d["W1"], d["b1"])
            edge_out(nc, t, d["W2"], d["b2"])
        graph_conv(nc, t, d["W_1"], d["gamma"], d["beta"], d["b_1"])
        with nc.sbuf_tensor("Sparts", [P, 3, PAIRS, P], BF16) as Sparts, nc.sbuf_tensor("gaps", [P, PAIRS, P, 3], BF16) as gaps:
            t.Sparts, t.gaps = Sparts, gaps
            sort_columns(nc, t)
            with nc.sbuf_tensor("agg", [P, B, C], F32) as agg:
                t.agg = agg
                quantiles(nc, t)
                quantile_out(nc, t, *(d["2" + n] for n in ("W1", "b1", "W2", "b2")))
        gru(nc, t, *(d["3" + n] for n in ("W1", "b1", "W2", "b2", "W_ih", "b_ih", "W_hh", "b_hh")))
        store(nc, t, out)


def store(nc, t, out):
    with nc.semaphore("stored") as stored, nc.Block() as block:
        @block.sync
        def _(sp):
            sp.dma_start(out, t.xs[:]).then_inc(stored, 16)
            sp.wait_ge(stored, 16)


def kernel(**inputs):
    import numpy as np
    import concourse.bacc as bacc
    from concourse.bass_utils import run_bass_kernel_spmd

    nc = bacc.Bacc("TRN2", target_bir_lowering=False, num_devices=1)
    a = {k: np.asarray(v) for k, v in inputs.items()}
    lay = lambda v: np.ascontiguousarray(v)
    col = lambda n: lay(a[n].reshape(-1, 1))
    vec = lambda n: lay(a[n].reshape(1, -1))
    host = {
        "x": lay(a["x"].transpose(1, 0, 2)),
        "xT": lay(a["x"].transpose(2, 0, 1).reshape(C, B * P)),
        "adj": lay(a["adj"].transpose(1, 0, 2)),
        "adjT": lay(a["adj"].transpose(2, 0, 1)),
        "mask": lay(a["nodemask"].T.view(np.uint8)),
        "ident": np.eye(P, dtype=np.float32),
        "W1": lay(a["L0_gnn_W1"].reshape(2, C, HID).transpose(1, 0, 2)),
        "b1": vec("L0_gnn_b1"),
        "W2": lay(a["L0_gnn_W2"]),
        "b2": vec("L0_gnn_b2"),
        "W_1": lay(a["L1_gnn_W"]), "gamma": vec("L1_gnn_gamma"), "beta": vec("L1_gnn_beta"), "b_1": vec("L1_gnn_b"),
        "2W1": lay(a["L2_gnn_W1"]), "2b1": col("L2_gnn_b1"), "2W2": lay(a["L2_gnn_W2"]), "2b2": vec("L2_gnn_b2"),
        "3W1": lay(a["L3_gnn_W1"]), "3b1": col("L3_gnn_b1"), "3W2": lay(a["L3_gnn_W2"]), "3b2": vec("L3_gnn_b2"),
        "3W_ih": lay(a["L3_gnn_W_ih"].T.reshape(C, 3, C)), "3b_ih": lay(a["L3_gnn_b_ih"].reshape(1, 3, C)),
        "3W_hh": lay(a["L3_gnn_W_hh"].T.reshape(C, 3, C)), "3b_hh": lay(a["L3_gnn_b_hh"].reshape(1, 3, C)),
    }
    d = {n: nc.dram_tensor("in_" + n, v.shape, mybir.dt.from_np(v.dtype), kind="ExternalInput").ap() for n, v in host.items()}
    out = nc.dram_tensor("out", (P, B, C), F32, kind="ExternalOutput").ap()
    for n in ("b2", "gamma", "beta", "b_1", "2b2", "3b2", "3b_ih", "3b_hh"):
        d[n] = d[n].broadcast_to([P, *d[n].shape[1:]])
    build(nc, d, out)
    r = run_bass_kernel_spmd(nc, [{"in_" + n: v for n, v in host.items()}], core_ids=[0])
    return lay(r.results[0]["out"].transpose(1, 0, 2))
```
